# Optimizing a Trainium2 kernel written in Bass

```python
import numpy as np
import jax
import jax.numpy as jnp

def _softmax(x, axis=-1):
    return jax.nn.softmax(x, axis=axis)

def _gelu(x):
    return jax.nn.gelu(x, approximate=True)

def _silu(x):
    return jax.nn.silu(x)

def _sigmoid(x):
    return jax.nn.sigmoid(x)

def _layernorm(x, axis=-1, eps=1e-05):
    m = jnp.mean(x, axis=axis, keepdims=True)
    v = jnp.var(x, axis=axis, keepdims=True)
    return (x - m) / jnp.sqrt(v + eps)

def _scatter_add(tgt, idx, src, axis=0):
    return tgt.at[idx].add(src)

def _segment_sum(src, seg, n):
    return jax.ops.segment_sum(src, seg, n)
kernel_name = 'mk_macaron_d1_jaxref_r4_0318c1'

def setup_inputs(seed: int=0):
    np.random.seed(seed)
    _w = jnp.asarray

    def _L0_attn_setup():
        import jax, jax.numpy as jnp
        import numpy as np
        NUM_HEADS = 16
        ROPE_BASE = 10000.0
        QK_GAIN_INIT = 12.0
        EPS = 1e-06
        ROPE_MASK = jnp.asarray(np.tile([1.0, 0.0], NUM_HEADS // 2), dtype=jnp.float32)

        def _rope_cos_sin(seqlen, head_dim, dtype):
            half = head_dim // 2
            inv_freq = ROPE_BASE ** (-jnp.arange(0, half, dtype=jnp.float32) / half)
            theta = jnp.arange(seqlen, dtype=jnp.float32)[:, None] * inv_freq[None, :]
            return (jnp.cos(theta).astype(dtype), jnp.sin(theta).astype(dtype))

        def _apply_rope(t, cos, sin):
            d2 = t.shape[-1] // 2
            t1, t2 = (t[..., :d2], t[..., d2:])
            c = cos[None, :, None, :]
            s = sin[None, :, None, :]
            return jnp.concatenate([t1 * c - t2 * s, t1 * s + t2 * c], axis=-1)

        def _unit_norm(t):
            return t * jax.lax.rsqrt(jnp.sum(t * t, axis=-1, keepdims=True) + EPS)
        key = jax.random.key(seed)
        k0, k1, k2 = jax.random.split(key, 3)
        B, S, Dm = (2, 512, 512)
        x = jax.random.normal(k0, (B, S, Dm), dtype=jnp.float32)
        w_qkv = jax.random.normal(k1, (Dm, 3 * Dm), dtype=jnp.float32) * Dm ** (-0.5)
        w_out = jax.random.normal(k2, (Dm, Dm), dtype=jnp.float32) * Dm ** (-0.5)
        q_gain = jnp.full((NUM_HEADS,), QK_GAIN_INIT, dtype=jnp.float32)
        return {'x': x, 'w_qkv': w_qkv, 'w_out': w_out, 'q_gain': q_gain}
    _L0_attn_in = _L0_attn_setup()

    def _L0_ffn_setup():
        import jax, jax.numpy as jnp
        import numpy as np
        DIM_IN = 512
        DIM_HIDDEN = 2048
        key = jax.random.key(seed)
        k_x, k_g, k_u, k_d = jax.random.split(key, 4)
        s_in = 1.0 / np.sqrt(DIM_IN)
        s_hid = 1.0 / np.sqrt(DIM_HIDDEN)
        x = jax.random.normal(k_x, (4, 512, DIM_IN), dtype=jnp.float32)
        w_gate = jax.random.uniform(k_g, (DIM_HIDDEN, DIM_IN), jnp.float32, -s_in, s_in)
        w_up = jax.random.uniform(k_u, (DIM_HIDDEN, DIM_IN), jnp.float32, -s_in, s_in)
        w_down = jax.random.uniform(k_d, (DIM_IN, DIM_HIDDEN), jnp.float32, -s_hid, s_hid)
        return {'x': x, 'w_gate': w_gate, 'w_up': w_up, 'w_down': w_down}
    _L0_ffn_in = _L0_ffn_setup()
    _d = {'L0_attn_x': _L0_attn_in['x'], 'L0_attn_w_qkv': _L0_attn_in['w_qkv'], 'L0_attn_w_out': _L0_attn_in['w_out'], 'L0_attn_q_gain': _L0_attn_in['q_gain'], 'L0_ffn_w_gate': _L0_ffn_in['w_gate'], 'L0_ffn_w_up': _L0_ffn_in['w_up'], 'L0_ffn_w_down': _L0_ffn_in['w_down']}
    _x0 = _d['L0_attn_x']
    _d['L0_attn_x'] = jax.random.normal(jax.random.fold_in(jax.random.key(seed), 1), (8, 512, 512), dtype=_x0.dtype)
    del _x0
    return _d

def reference(L0_attn_x, L0_attn_w_qkv, L0_attn_w_out, L0_attn_q_gain, L0_ffn_w_gate, L0_ffn_w_up, L0_ffn_w_down):

    def _L0_attn_ref(x, w_qkv, w_out, q_gain):
        import jax, jax.numpy as jnp
        import numpy as np
        NUM_HEADS = 16
        ROPE_BASE = 10000.0
        QK_GAIN_INIT = 12.0
        EPS = 1e-06
        ROPE_MASK = jnp.asarray(np.tile([1.0, 0.0], NUM_HEADS // 2), dtype=jnp.float32)

        def _rope_cos_sin(seqlen, head_dim, dtype):
            half = head_dim // 2
            inv_freq = ROPE_BASE ** (-jnp.arange(0, half, dtype=jnp.float32) / half)
            theta = jnp.arange(seqlen, dtype=jnp.float32)[:, None] * inv_freq[None, :]
            return (jnp.cos(theta).astype(dtype), jnp.sin(theta).astype(dtype))

        def _apply_rope(t, cos, sin):
            d2 = t.shape[-1] // 2
            t1, t2 = (t[..., :d2], t[..., d2:])
            c = cos[None, :, None, :]
            s = sin[None, :, None, :]
            return jnp.concatenate([t1 * c - t2 * s, t1 * s + t2 * c], axis=-1)

        def _unit_norm(t):
            return t * jax.lax.rsqrt(jnp.sum(t * t, axis=-1, keepdims=True) + EPS)
        B, S, Dm = x.shape
        H = NUM_HEADS
        D = Dm // H
        qkv = (x @ w_qkv).reshape(B, S, 3, H, D)
        q, k, v = (qkv[:, :, 0], qkv[:, :, 1], qkv[:, :, 2])
        q = _unit_norm(q)
        k = _unit_norm(k)
        cos, sin = _rope_cos_sin(S, D, x.dtype)
        m = ROPE_MASK[None, None, :, None]
        q = m * _apply_rope(q, cos, sin) + (1.0 - m) * q
        k = m * _apply_rope(k, cos, sin) + (1.0 - m) * k
        logits = jnp.einsum('bshd,bthd->bhst', q, k) * q_gain[None, :, None, None]
        causal = jnp.tril(jnp.ones((S, S), dtype=bool))
        logits = jnp.where(causal[None, None], logits, jnp.finfo(logits.dtype).min)
        attn = jax.nn.softmax(logits, axis=-1)
        y = jnp.einsum('bhst,bthd->bshd', attn, v).reshape(B, S, Dm)
        return y @ w_out

    def _L0_ffn_ref(x, w_gate, w_up, w_down):
        import jax, jax.numpy as jnp
        import numpy as np
        DIM_IN = 512
        DIM_HIDDEN = 2048
        gate = jnp.einsum('bsd,hd->bsh', x, w_gate)
        up = jnp.einsum('bsd,hd->bsh', x, w_up)
        gated = jax.nn.silu(gate) * up
        return jnp.einsum('bsh,dh->bsd', gated, w_down)
    x = L0_attn_x
    x = x + 0.5 * _L0_ffn_ref(_layernorm(x, axis=-1), L0_ffn_w_gate, L0_ffn_w_up, L0_ffn_w_down)
    x = x + _L0_attn_ref(_layernorm(x, axis=-1), L0_attn_w_qkv, L0_attn_w_out, L0_attn_q_gain)
    x = x + 0.5 * _L0_ffn_ref(_layernorm(x, axis=-1), L0_ffn_w_gate, L0_ffn_w_up, L0_ffn_w_down)
    return x

_drawn_inputs = setup_inputs


def setup_inputs(seed=0):
    import zlib

    import numpy as np

    out = dict(_drawn_inputs(seed))
    spreads = {'L0_attn_q_gain': (12.0, 0.2)}
    factors = {}
    for name, (base, spread) in spreads.items():
        noise = np.random.default_rng([zlib.crc32(name.encode()), seed]).standard_normal(out[name].shape)
        drawn = base * np.exp(spread * noise) if base else spread * noise
        out[name] = jnp.asarray(drawn.astype(out[name].dtype))
    for name, factor in factors.items():
        out[name] = (out[name] * factor).astype(out[name].dtype)
    return out
```

```python
import concourse.bass as bass
from concourse import mybir
from concourse.alu_op_type import AluOpType as ALU

ACT = mybir.ActivationFunctionType
AX_X = mybir.AxisListType.X
RMAX = bass.bass_isa.ReduceOp.max
F32, F16, BF16, I32 = mybir.dt.float32, mybir.dt.float16, mybir.dt.bfloat16, mybir.dt.int32

P = 128
B, S, D, H = 8, 512, 512, 16
HD = D // H
HID = 2048
KC = D // P
TT = S // P
HC = HID // P
HH = H // 2
GH = 4
ST = 3 * HD
MR = 2 * GH
VW = 2 * HD + 2
YW = 2 * HD + 1
SW = P * TT * (TT + 1) // 2
LN_EPS, QK_EPS = 1e-5, 1e-6
LEAST = 2.0 ** -60
MASKED = -1e36
EXP_BITS = 0x7F800000
LN2 = 0.6931471805599453


def build(nc, x, w_qkv, w_out, q_gain, w_gate, w_up, w_down, rope, out):
    def sb(name, cols, dt):
        return nc.alloc_sbuf_tensor(name, [P, cols], dt)

    WG = sb("WG", 2 * KC * HID, F16)[:, :].rearrange("p (s k n) -> p s k n", s=2, k=KC)
    WU = sb("WU", 2 * KC * HID, F16)[:, :].rearrange("p (s k n) -> p s k n", s=2, k=KC)
    WD = sb("WD", 2 * HC * D, F16)[:, :].rearrange("p (s k n) -> p s k n", s=2, k=HC)
    WQ = sb("WQ", 2 * KC * 3 * D, F16)[:, :].rearrange("p (s k n) -> p s k n", s=2, k=KC)
    WO = sb("WO", 2 * KC * D, F16)[:, :].rearrange("p (s k n) -> p s k n", s=2, k=KC)

    at, place = 0, {}
    for name, words in (("xin", TT * D), ("xres", TT * D), ("xt", KC * S), ("qt", HH * S // 2),
                        ("kt", HH * S // 2), ("v", TT * HH * VW // 2), ("work", 5120),
                        ("ysb", GH * TT * YW), ("yf", TT * P)):
        place[name] = (at, words)
        at += words
    arena = sb("arena", at, F32)

    def words(name, first=0, n=None):
        a, size = place[name]
        n = size - first if n is None else n
        return arena[:, a + first:a + first + n]

    def halves(name, first=0, n=None):
        return words(name, first, n).bitcast(F16)

    xin = words("xin").rearrange("p (t d) -> p t d", t=TT)
    xres = words("xres").rearrange("p (t d) -> p t d", t=TT)
    XT = halves("xt").rearrange("p (s k n) -> p s k n", s=2, k=KC)
    YT = halves("xin").rearrange("p (s k n) -> p s k n", s=2, k=KC)
    xn = words("qt").rearrange("p (t d) -> p t d", t=TT)
    QT = halves("qt").rearrange("p (h n) -> p h n", h=HH)
    KT = halves("kt").rearrange("p (h n) -> p h n", h=HH)
    V = halves("v").rearrange("p (t h c) -> p t h c", t=TT, h=HH)
    P32 = [words("work", SW * i, SW) for i in range(2)]
    PHI = [halves("work", 2 * SW + SW // 2 * i, SW // 2) for i in range(2)]
    PLO = [halves("work", 3 * SW + SW // 2 * i, SW // 2) for i in range(2)]
    Ysb = words("ysb").rearrange("p (h t c) -> p h t c", h=GH, t=TT)
    Yf = words("yf").rearrange("p (t h c) -> p t h c", t=TT, h=GH)
    qs = [words("work", D * i, D) for i in range(2)]
    sq = [words("work", 2 * D + D * i, D) for i in range(2)]
    qn = [words("work", 4 * D + D * i, D) for i in range(2)]
    ropeU = words("work", 6 * D, D // 2)
    ropeV = words("work", 6 * D + D // 2, D // 2)
    STK = [halves("work", 7 * D + HH * ST * i, HH * ST).rearrange("p (h c) -> p h c", h=2 * HH) for i in range(2)]
    fT = [words("work", S * i, S) for i in range(2)]
    fA = words("work", 2 * S, S)
    fH = [words("work", 3 * S + S * i, S) for i in range(2)]
    Hhi = [halves("work", 5 * S + S // 2 * i, S // 2) for i in range(2)]
    Hlo = [halves("work", 6 * S + S // 2 * i, S // 2) for i in range(2)]
    RAW = [arena[:, 2048 * (i + 1):2048 * (i + 2)].rearrange("p (i d) -> p i d", i=4) for i in range(4)]
    w0 = place["work"][0]
    RAWD = [arena[:, 0:2048]] + [arena[:, w0 + 2048 * i:w0 + 2048 * (i + 1)] for i in range(3)]
    WD32 = arena[:, 2048:2048 + HC * D]
    RAWQ = arena[:, w0:w0 + KC * 3 * D]
    RAWO = arena[:, 0:KC * D]

    ident = sb("ident", P, F32)
    ident16 = sb("ident16", P, F16)
    identb = sb("identb", P, BF16)
    maskq = sb("maskq", P, BF16)
    maskk = sb("maskk", P, BF16)
    ropet = sb("ropet", TT * 64, F32)
    ropev = ropet[:, :].rearrange("p (t c) -> p t c", t=TT)
    gain = sb("gain", 5 * H, F32)
    hscale = sb("hscale", H, F32)
    wmax = sb("wmax", 32, F32)
    wpow = sb("wpow", 32, F32)
    wrec = sb("wrec", 32, F32)
    wscale = sb("wscale", 32, F32)
    tscale = sb("tscale", HC, F32)
    pgu = sb("pgu", HC, F32)
    gmax = sb("gmax", 3, F32)
    gall = sb("gall", 3, F32)
    gpow = sb("gpow", 3, F32)
    grec = sb("grec", 3, F32)
    gscale = sb("gscale", 3, F32)
    unscale = sb("unscale", 4, F32)
    stats = sb("stats", 6 * TT, F32)
    mv = sb("mv", 2 * TT, F32)
    var2 = sb("var2", TT, F32)
    rstd = sb("rstd", TT, F32)
    mhalf = sb("mhalf", 2 * HH, F32)
    ss = sb("ss", 4 * HH, F32)
    ss2 = sb("ss2", 4 * HH, F32)
    rn = sb("rn", 4 * HH, F32)
    mneg = sb("mneg", TT * HH, F32)
    mst = sb("mst", TT * MR, F16)
    yrec = sb("yrec", GH * TT, F32)
    carrier = sb("carrier", HH + 3 * TT, F32)
    lnbias = sb("lnbias", 1, F32)

    psum = nc.alloc_psum_tensor("psum", [P, 8 * 512], F32)

    def ps(b, a=0, n=512):
        return psum[:, b * 512 + a:b * 512 + a + n]

    def ps16(b):
        return psum[:, b * 512:(b + 1) * 512].bitcast(F16)

    QSEG = {3: 0, 2: 512, 0: 896, 1: 1024}
    KSEG = {0: 0, 1: 512, 3: 896, 2: 1024}

    names = """c_in raw0 raw1 raw2 raw3 down_in qkv_in out_in c_made wscaled wsent w_tr w_hi w_lo
        dn_tr dn_st gmax_in gmax_all scales wd_hi wd_lo sel_done pro_hi pro_lo
        x_loaded x_stored out_ready var_ready rstd_ready xn_done xt_ps xt_hi xt_lo
        g_ps u_ps tanh_done gated h_hi h_lo down_done acc_done
        qk_ps v_ps qs_done sq_done vhi_done vlo_done ssq_ready r_ready qn_done rope_done
        st_hi st_lo qt_ps kt_ps qt_ev kt_ev s1_ps smax_done mst_done mt_ps mt_copied mrow_done
        s2_ps exp_done phi_done plo_done pv_ps y_copied ynorm_done yt_ps yt_hi yt_lo op_ps
        dve_chain dve_a pool_chain pool_pro dve_pro"""
    s = {n: nc.alloc_semaphore(n) for n in names.split()}

    def per(eng, it):
        def wait(name, n, k):
            eng.wait_ge(s[name], it * n + k)
        return wait

    with nc.Block() as block:

        @block.sync
        def _(sp):
            sp.sem_inc(s["x_stored"], 1)
            sp.dma_start(ropev, rope.rearrange("(t p) c -> p t c", p=P)).then_inc(s["c_in"], 16)
            sp.dma_start(gain[:, 0:H], q_gain.rearrange("(a n) -> a n", a=1).broadcast_to([P, H])).then_inc(s["c_in"], 16)
            for j in range(8):
                w = (w_gate if j < 4 else w_up)[(j % 4) * 512:(j % 4 + 1) * 512, :]
                if j >= 4:
                    sp.wait_ge(s["w_tr"], j - 3)
                sp.dma_start(RAW[j % 4], w.rearrange("(i p) d -> p i d", p=P)).then_inc(s[f"raw{j % 4}"], 16)
                if j == 3:
                    for t in range(4):
                        sp.dma_start(RAWD[t], w_down[t * P:(t + 1) * P, :]).then_inc(s["down_in"], 16)
            sp.wait_ge(s["dn_tr"], 16)
            sp.dma_start(RAWQ.rearrange("p (k n) -> p k n", k=KC), w_qkv.rearrange("(k p) n -> p k n", p=P)).then_inc(s["qkv_in"], 16)
            sp.dma_start(RAWO.rearrange("p (k n) -> p k n", k=KC), w_out.rearrange("(k p) n -> p k n", p=P)).then_inc(s["out_in"], 16)
            sp.wait_ge(s["pro_lo"], 2)
            sp.wait_ge(s["pro_hi"], 2)
            sp.dma_start(xin, x[0].rearrange("(t p) d -> p t d", p=P)).then_inc(s["x_loaded"], 16)
            with sp.Fori(0, B - 1) as it:
                wait = per(sp, it)
                wait("op_ps", TT, TT)
                sp.dma_start(xin, x[it + 1].rearrange("(t p) d -> p t d", p=P)).then_inc(s["x_loaded"], 16)
                wait("out_ready", TT, TT)
                sp.dma_start(out[it].rearrange("(t p) d -> p t d", p=P), xres).then_inc(s["x_stored"], 16)
            sp.wait_ge(s["out_ready"], B * TT)
            sp.dma_start(out[B - 1].rearrange("(t p) d -> p t d", p=P), xres).then_inc(s["x_stored"], 16)
            sp.wait_ge(s["x_stored"], 16 * B + 1)

        @block.gpsimd
        def _(pool):
            n = [0]

            def link(ins):
                n[0] += 1
                ins.then_inc(s["pool_pro"], 1)
                pool.wait_ge(s["pool_pro"], n[0])

            for m in (ident, ident16, identb, maskq, maskk):
                link(nc.gpsimd.memset(m[:, :], 0.0))
            link(nc.gpsimd.memset(mhalf[:, :], -0.5))
            link(nc.gpsimd.memset(mst[:, :], 0.0))
            link(nc.gpsimd.memset(halves("v"), 1.0))
            for m in (ident, ident16, identb):
                link(nc.gpsimd.affine_select(out=m[:, :], in_=m[:, :], compare_op=ALU.not_equal, fill=1.0,
                                             base=0, pattern=[[-1, P]], channel_multiplier=1))
            link(nc.gpsimd.affine_select(out=maskq[:, :], in_=maskq[:, :], compare_op=ALU.is_ge, fill=MASKED,
                                         base=0, pattern=[[-1, P]], channel_multiplier=1))
            nc.gpsimd.affine_select(out=maskk[:, :], in_=maskk[:, :], compare_op=ALU.is_ge, fill=MASKED,
                                    base=0, pattern=[[1, P]], channel_multiplier=-1).then_inc(s["c_made"], 1)
            pool.wait_ge(s["gmax_in"], 3)
            nc.gpsimd.partition_all_reduce(gall[:, :], gmax[:, :], P, RMAX).then_inc(s["gmax_all"], 1)
            pool.wait_ge(s["wd_lo"], 4)
            kr = KT[ST:ST + MR, :, :]
            link(nc.gpsimd.memset(kr, 4096.0))
            krv = KT[ST:ST + MR, :, :].rearrange("p (a g) n -> p a g n", g=GH)
            link(nc.gpsimd.affine_select(out=krv, in_=krv, compare_op=ALU.is_ge, fill=0.0, base=0,
                                         pattern=[[0, 2], [-2, GH], [0, S]], channel_multiplier=1))
            nc.gpsimd.affine_select(out=krv, in_=krv, compare_op=ALU.is_ge, fill=0.0, base=1,
                                    pattern=[[0, 2], [2, GH], [0, S]], channel_multiplier=-1).then_inc(s["sel_done"], 1)
            pool.wait_ge(s["sel_done"], 1)

            with pool.Fori(0, B) as it:
                wait = per(pool, it)

                def rsqrt_of_variance(u):
                    for t in range(TT):
                        wait("var_ready", 12, 4 * u + t + 1)
                        nc.gpsimd.tensor_tensor(rstd[:, t:t + 1], var2[:, t:t + 1], mhalf[:, 0:1], ALU.pow).then_inc(s["rstd_ready"], 1)

                rsqrt_of_variance(0)
                rsqrt_of_variance(1)
                nr = [0]
                for hf in range(2):
                    for t in range(TT):
                        i, b2 = hf * TT + t, t % 2
                        wait("ssq_ready", 8, i + 1)
                        nc.gpsimd.tensor_tensor(rn[:, 16 * b2:16 * b2 + 16], ss2[:, 16 * b2:16 * b2 + 16], mhalf[:, :], ALU.pow).then_inc(s["r_ready"], 1)
                        wait("qn_done", 8, i + 1)
                        ev = qn[b2].rearrange("p (e o c) -> p e o c", o=2, c=HD)[:, :, 0, :]
                        U = ropeU.rearrange("p (e c) -> p e c", c=HD)
                        Vv = ropeV.rearrange("p (e c) -> p e c", c=HD)
                        hw = HD // 2
                        bc = lambda a, w: ropev[:, t, a:a + w].unsqueeze(1).broadcast_to([P, HH, w])
                        nc.gpsimd.tensor_tensor(U, ev, bc(0, HD), ALU.mult)
                        nc.gpsimd.tensor_tensor(Vv[:, :, 0:hw], ev[:, :, hw:HD], bc(HD, hw), ALU.mult)
                        nr[0] += 1
                        nc.gpsimd.tensor_tensor(Vv[:, :, hw:HD], ev[:, :, 0:hw], bc(HD + hw, hw), ALU.mult).then_inc(s["pool_chain"], 1)
                        wait("pool_chain", 8, nr[0])
                        nc.gpsimd.tensor_tensor(ev, U, Vv, ALU.add).then_inc(s["rope_done"], 1)
                    for h in range(HH):
                        k = hf * HH + h
                        wait("exp_done", 16, k + 1)
                        if h >= 2:
                            wait("pv_ps", 16, k - 1)
                        nc.gpsimd.tensor_tensor(carrier[:, h:h + 1], mhalf[:, 0:1], mhalf[:, 0:1], ALU.mult)
                        nc.gpsimd.tensor_scalar(PHI[h % 2], P32[h % 2], 1.0, None, ALU.mult).then_inc(s["phi_done"], 1)
                rsqrt_of_variance(2)

        @block.scalar
        def _(act):
            for j in range(8):
                r = RAW[j % 4]
                act.wait_ge(s["wsent"], j + 1)
                for i in range(4):
                    c = 4 * j + i
                    ins = nc.scalar.activation(r[:, i, :], r[:, i, :], ACT.Copy, scale=wscale[:, c:c + 1])
                ins.then_inc(s["wscaled"], 1)
                act.wait_ge(s["w_tr"], j + 1)
                W = WG if j < 4 else WU
                for k in range(KC):
                    nc.scalar.activation(W[:, 0, k, (j % 4) * 512:(j % 4 + 1) * 512], ps((j % 2) * 4 + k), ACT.Copy).then_inc(s["w_hi"], 1)
            act.wait_ge(s["scales"], 1)
            for q in range(4):
                nc.scalar.activation(WD[:, 0, 4 * q:4 * q + 4, :], WD32[:, 2048 * q:2048 * (q + 1)].rearrange("p (k n) -> p k n", n=D),
                                     ACT.Copy, scale=gscale[:, 0:1]).then_inc(s["wd_hi"], 1)
            nc.scalar.activation(WQ[:, 0], RAWQ.rearrange("p (k n) -> p k n", k=KC), ACT.Copy, scale=gscale[:, 1:2]).then_inc(s["pro_hi"], 1)
            nc.scalar.activation(WO[:, 0], RAWO.rearrange("p (k n) -> p k n", k=KC), ACT.Copy, scale=gscale[:, 2:3]).then_inc(s["pro_hi"], 1)

            with act.Fori(0, B) as it:
                wait = per(act, it)

                def xt_hi(u):
                    for k in range(KC):
                        wait("xt_ps", 12, 4 * u + k + 1)
                        nc.scalar.activation(XT[:, 0, k, :], ps(4 + k), ACT.Copy).then_inc(s["xt_hi"], 1)

                def ffn(f):
                    for c in range(HC):
                        k = f * HC + c
                        wait("g_ps", 32, k + 1)
                        nc.scalar.activation(fT[c % 2], ps(4 + 2 * (c % 2)), ACT.Tanh, scale=tscale[:, c:c + 1]).then_inc(s["tanh_done"], 1)
                        wait("gated", 32, k + 1)
                        if c >= 2:
                            wait("down_done", 2 * (HC - 1), f * (HC - 1) + c - 1)
                        nc.scalar.activation(Hhi[c % 2], fH[c % 2], ACT.Copy).then_inc(s["h_hi"], 1)

                def qkv_in(hf, t):
                    i, b2 = hf * TT + t, t % 2
                    wait("qk_ps", 8, i + 1)
                    if t >= 2:
                        wait("qn_done", 8, i - 1)
                    nc.scalar.activation(qs[b2], ps(2 * b2), ACT.Copy, scale=unscale[:, 1:2]).then_inc(s["qs_done"], 1)
                    nc.scalar.activation(sq[b2], ps(2 * b2), ACT.Square, scale=unscale[:, 1:2]).then_inc(s["sq_done"], 1)
                    wait("v_ps", 8, i + 1)
                    nc.scalar.activation(V[:, t, :, HD:2 * HD], ps(2 * b2 + 1, 0, 256).rearrange("p (h c) -> p h c", c=HD),
                                         ACT.Copy, scale=2.0 ** -17).then_inc(s["vhi_done"], 1)

                def stack_hi(hf, t):
                    i, b2 = hf * TT + t, t % 2
                    wait("rope_done", 8, i + 1)
                    if t >= 2:
                        wait("kt_ps", 8, i - 1)
                    q3 = qn[b2].rearrange("p (h c) -> p h c", c=HD)
                    nc.scalar.activation(STK[b2][:, :, 0:HD], q3, ACT.Copy)
                    nc.scalar.activation(STK[b2][:, 0:HH, HD:2 * HD], q3[:, 0:HH, :], ACT.Copy)
                    nc.scalar.activation(STK[b2][:, HH:2 * HH, 2 * HD:ST], q3[:, HH:2 * HH, :], ACT.Copy).then_inc(s["st_hi"], 1)

                def qt_out(hf, t):
                    i, b2 = hf * TT + t, t % 2
                    wait("qt_ps", 8, i + 1)
                    nc.scalar.activation(QT[0:ST, :, t * P:(t + 1) * P], ps16(4 + 2 * b2)[0:ST, :].rearrange("p (h n) -> p h n", h=HH),
                                         ACT.Copy).then_inc(s["qt_ev"], 1)

                def max_rows(hf, g):
                    k = hf * 2 + g
                    wait("mt_ps", 4, k + 1)
                    nc.scalar.activation(QT[ST:ST + MR, g * GH, :], ps16(7)[ST:ST + MR, 0:S], ACT.Copy).then_inc(s["mt_copied"], 1)

                def exp(hf, h):
                    k = hf * HH + h
                    wait("s2_ps", 16, k + 1)
                    if h >= 2:
                        wait("plo_done", 16, k - 1)
                    nc.scalar.activation(P32[h % 2], ps(3, 0, SW), ACT.Exp, bias=lnbias[:, 0:1],
                                         scale=hscale[:, k:k + 1]).then_inc(s["exp_done"], 1)

                def y_out(hf, h):
                    k = hf * HH + h
                    wait("pv_ps", 16, k + 1)
                    if h % GH == 0 and k > 0:
                        wait("ynorm_done", 4, k // GH)
                    nc.scalar.activation(Ysb[:, h % GH], ps(6, 0, TT * YW).rearrange("p (t c) -> p t c", t=TT), ACT.Copy).then_inc(s["y_copied"], 1)

                def yt_hi(hf, g):
                    k = hf * 2 + g
                    wait("yt_ps", 4, k + 1)
                    nc.scalar.activation(YT[:, 0, k, :], ps(7), ACT.Copy).then_inc(s["yt_hi"], 1)

                xt_hi(0)
                ffn(0)
                xt_hi(1)
                for hf in range(2):
                    qkv_in(hf, 0)
                    for t in range(TT):
                        if t + 1 < TT:
                            qkv_in(hf, t + 1)
                        stack_hi(hf, t)
                        qt_out(hf, t)
                    max_rows(hf, 0)
                    for h in range(HH):
                        if h == GH:
                            max_rows(hf, 1)
                        exp(hf, h)
                        if h >= 1:
                            y_out(hf, h - 1)
                        if h == 5:
                            yt_hi(hf, 0)
                    y_out(hf, HH - 1)
                    yt_hi(hf, 1)
                xt_hi(2)
                ffn(1)

        @block.vector
        def _(dve):
            V_ = nc.vector
            n = [0]

            def link(ins):
                n[0] += 1
                ins.then_inc(s["dve_pro"], 1)
                dve.wait_ge(s["dve_pro"], n[0])

            def power_of_two(out, in_):
                link(V_.tensor_scalar(out, in_, LEAST, None, ALU.max))
                link(V_.tensor_scalar(out.bitcast(I32), out.bitcast(I32), EXP_BITS, None, ALU.bitwise_and))

            link(V_.memset(lnbias[:, :], 14 * LN2))
            dve.wait_ge(s["c_in"], 32)
            g0, g1, g2, g3, g4 = (gain[:, i * H:(i + 1) * H] for i in range(5))
            link(V_.tensor_scalar(g1.bitcast(I32), g0.bitcast(I32), 0x7FFFFFFF, None, ALU.bitwise_and))
            power_of_two(g2, g1)
            link(V_.reciprocal(g3, g2))
            link(V_.tensor_tensor(g4, g0, g3, ALU.mult))
            link(V_.tensor_scalar(hscale[:, :], g2, 2.0 ** -24, None, ALU.mult))

            def w_scales(j):
                c = slice(4 * j, 4 * j + 4)
                dve.wait_ge(s[f"raw{j % 4}"], 16 * (j // 4 + 1))
                link(V_.tensor_reduce(wmax[:, c], RAW[j % 4], AX_X, ALU.max, apply_absolute_value=True))
                power_of_two(wpow[:, c], wmax[:, c])
                link(V_.reciprocal(wrec[:, c], wpow[:, c]))
                V_.tensor_scalar(wscale[:, c], wrec[:, c], 2.0 ** 13, None, ALU.mult).then_inc(s["wsent"], 1)

            w_scales(0)
            for j in range(8):
                if j + 1 < 8:
                    w_scales(j + 1)
                W = WG if j < 4 else WU
                for k in range(KC):
                    dve.wait_ge(s["w_hi"], 4 * j + k + 1)
                    c = slice((j % 4) * 512, (j % 4 + 1) * 512)
                    V_.tensor_tensor(W[:, 1, k, c], ps((j % 2) * 4 + k), W[:, 0, k, c], ALU.subtract).then_inc(s["w_lo"], 1)
            link(V_.tensor_scalar(tscale[:, :], wpow[:, 0:HC], 2.0 ** -23, None, ALU.mult))
            link(V_.scalar_tensor_tensor(out=pgu[:, :], in0=wpow[:, 0:HC], scalar=2.0 ** 5, in1=wpow[:, HC:2 * HC], op0=ALU.mult, op1=ALU.mult))
            WD32v = WD32.rearrange("p (k n) -> p k n", n=D)
            for m in range(16):
                q, t = m // 4, m % 4
                dve.wait_ge(s["dn_tr"], m + 1)
                ins = V_.tensor_tensor(WD32v[:, 4 * q:4 * q + 4, t * P:(t + 1) * P], ps(m % 8).rearrange("p (k n) -> p k n", n=P),
                                       pgu[:, 4 * q:4 * q + 4].unsqueeze(2).broadcast_to([P, 4, P]), ALU.mult)
                ins.then_inc(s["dn_st"], 1)
            dve.wait_ge(s["dn_st"], 16)
            V_.tensor_reduce(gmax[:, 0:1], WD32, AX_X, ALU.max, apply_absolute_value=True).then_inc(s["gmax_in"], 1)
            dve.wait_ge(s["qkv_in"], 16)
            V_.tensor_reduce(gmax[:, 1:2], RAWQ, AX_X, ALU.max, apply_absolute_value=True).then_inc(s["gmax_in"], 1)
            dve.wait_ge(s["out_in"], 16)
            V_.tensor_reduce(gmax[:, 2:3], RAWO, AX_X, ALU.max, apply_absolute_value=True).then_inc(s["gmax_in"], 1)
            dve.wait_ge(s["gmax_all"], 1)
            power_of_two(gpow[:, :], gall[:, :])
            link(V_.reciprocal(grec[:, :], gpow[:, :]))
            link(V_.tensor_scalar(unscale[:, 0:1], gpow[:, 0:1], 2.0 ** -14, None, ALU.mult))
            link(V_.tensor_scalar(unscale[:, 1:2], gpow[:, 1:2], 2.0 ** -22, None, ALU.mult))
            link(V_.scalar_tensor_tensor(out=unscale[:, 2:3], in0=gpow[:, 1:2], scalar=2.0 ** -18, in1=gpow[:, 2:3], op0=ALU.mult, op1=ALU.mult))
            V_.tensor_scalar(gscale[:, :], grec[:, :], 2.0 ** 13, None, ALU.mult).then_inc(s["scales"], 1)
            dve.wait_ge(s["scales"], 1)
            for q in range(4):
                dve.wait_ge(s["wd_hi"], q + 1)
                V_.scalar_tensor_tensor(out=WD[:, 1, 4 * q:4 * q + 4, :].rearrange("p k n -> p (k n)"), in0=WD32[:, 2048 * q:2048 * (q + 1)], scalar=gscale[:, 0:1],
                                        in1=WD[:, 0, 4 * q:4 * q + 4, :].rearrange("p k n -> p (k n)"), op0=ALU.mult, op1=ALU.subtract).then_inc(s["wd_lo"], 1)
            for W, raw, c, m in ((WQ, RAWQ, 1, 1), (WO, RAWO, 2, 2)):
                dve.wait_ge(s["pro_hi"], m)
                V_.scalar_tensor_tensor(out=W[:, 1].rearrange("p k n -> p (k n)"), in0=raw, scalar=gscale[:, c:c + 1],
                                        in1=W[:, 0].rearrange("p k n -> p (k n)"), op0=ALU.mult, op1=ALU.subtract).then_inc(s["pro_lo"], 1)

            LINKS = 3 * TT * 2 + 2 * TT + 2 * TT * 2 + 4 + 4 * 2
            with dve.Fori(0, B) as it:
                wait = per(dve, it)
                n = [0]

                def link(ins):
                    n[0] += 1
                    ins.then_inc(s["dve_chain"], 1)
                    wait("dve_chain", LINKS, n[0])

                def norm_stats(u, t, src):
                    n[0] += 1
                    V_.bn_stats(stats[:, 6 * t:6 * t + 6], src[:, t, :]).then_inc(s["dve_chain"], 1)
                    wait("dve_chain", LINKS, n[0])
                    V_.memset(carrier[:, HH + 4 * u + t:HH + 4 * u + t + 1], 0.0)
                    link(V_.bn_aggr(mv[:, 2 * t:2 * t + 2], stats[:, 6 * t:6 * t + 6]))
                    V_.tensor_scalar(var2[:, t:t + 1], mv[:, 2 * t + 1:2 * t + 2], LN_EPS, 2.0 ** -18, ALU.add, ALU.mult).then_inc(s["var_ready"], 1)

                def norm_out(u, t, src):
                    wait("rstd_ready", 12, 4 * u + t + 1)
                    V_.tensor_scalar(xn[:, t, :], src[:, t, :], mv[:, 2 * t:2 * t + 1], rstd[:, t:t + 1], ALU.subtract, ALU.mult).then_inc(s["xn_done"], 1)

                def xt_lo(u):
                    for k in range(KC):
                        wait("xt_hi", 12, 4 * u + k + 1)
                        V_.tensor_tensor(XT[:, 1, k, :], ps(4 + k), XT[:, 0, k, :], ALU.subtract).then_inc(s["xt_lo"], 1)

                def ffn(f):
                    for c in range(HC):
                        k = f * HC + c
                        wait("tanh_done", 32, k + 1)
                        V_.scalar_tensor_tensor(out=fA, in0=fT[c % 2], scalar=1.0, in1=ps(4 + 2 * (c % 2)), op0=ALU.add, op1=ALU.mult).then_inc(s["dve_a"], 1)
                        wait("dve_a", 32, k + 1)
                        wait("u_ps", 32, k + 1)
                        V_.scalar_tensor_tensor(out=fH[c % 2], in0=fA, scalar=2.0 ** -50, in1=ps(5 + 2 * (c % 2)), op0=ALU.mult, op1=ALU.mult).then_inc(s["gated"], 1)
                        wait("h_hi", 32, k + 1)
                        V_.tensor_tensor(Hlo[c % 2], fH[c % 2], Hhi[c % 2], ALU.subtract).then_inc(s["h_lo"], 1)

                wait("x_loaded", 16, 16)
                for t in range(TT):
                    norm_stats(0, t, xin)
                    if t:
                        norm_out(0, t - 1, xin)
                norm_out(0, TT - 1, xin)
                xt_lo(0)
                ffn(0)
                wait("x_stored", 16, 1)
                for t in range(TT):
                    wait("acc_done", 8, t + 1)
                    link(V_.scalar_tensor_tensor(out=xres[:, t, :], in0=ps(t), scalar=unscale[:, 0:1], in1=xin[:, t, :], op0=ALU.mult, op1=ALU.add))
                    norm_stats(1, t, xres)
                    if t:
                        norm_out(1, t - 1, xres)
                norm_out(1, TT - 1, xres)
                xt_lo(1)

                def tile_norms(hf, t):
                    i, b2 = hf * TT + t, t % 2
                    c = slice(16 * b2, 16 * b2 + 16)
                    wait("sq_done", 8, i + 1)
                    link(V_.tensor_reduce(ss[:, c], sq[b2].rearrange("p (h c) -> p h c", c=HD), AX_X, ALU.add))
                    V_.tensor_scalar(ss2[:, c], ss[:, c], QK_EPS, 2.0 ** -24, ALU.add, ALU.mult).then_inc(s["ssq_ready"], 1)
                    wait("vhi_done", 8, i + 1)
                    V_.scalar_tensor_tensor(out=V[:, t, :, 0:HD], in0=ps(2 * b2 + 1, 0, 256).rearrange("p (h c) -> p h c", c=HD), scalar=2.0 ** -17,
                                            in1=V[:, t, :, HD:2 * HD], op0=ALU.mult, op1=ALU.subtract).then_inc(s["vlo_done"], 1)
                    wait("r_ready", 8, i + 1)
                    link(V_.tensor_tensor(rn[:, 16 * b2:16 * b2 + HH], rn[:, 16 * b2:16 * b2 + HH], gain[:, 4 * H + hf * HH:4 * H + (hf + 1) * HH], ALU.mult))
                    V_.tensor_tensor(qn[b2].rearrange("p (h c) -> p h c", c=HD), qs[b2].rearrange("p (h c) -> p h c", c=HD),
                                     rn[:, c].unsqueeze(2).broadcast_to([P, 2 * HH, HD]), ALU.mult).then_inc(s["qn_done"], 1)

                def stack_lo(hf, t):
                    i, b2 = hf * TT + t, t % 2
                    wait("st_hi", 8, i + 1)
                    q3 = qn[b2].rearrange("p (h c) -> p h c", c=HD)
                    V_.tensor_tensor(STK[b2][:, 0:HH, 2 * HD:ST], q3[:, 0:HH, :], STK[b2][:, 0:HH, 0:HD], ALU.subtract)
                    V_.tensor_tensor(STK[b2][:, HH:2 * HH, HD:2 * HD], q3[:, HH:2 * HH, :], STK[b2][:, HH:2 * HH, 0:HD], ALU.subtract).then_inc(s["st_lo"], 1)

                def kt_out(hf, t):
                    i, b2 = hf * TT + t, t % 2
                    wait("kt_ps", 8, i + 1)
                    V_.tensor_copy(KT[0:ST, :, t * P:(t + 1) * P], ps16(5 + 2 * b2)[0:ST, :].rearrange("p (h n) -> p h n", h=HH)).then_inc(s["kt_ev"], 1)

                mnegv = mneg[:, :].rearrange("p (t h) -> p t h", t=TT)
                mstv = mst[:, :].rearrange("p (t h c) -> p t h c", t=TT, c=2)

                def row_max(hf, h):
                    k = hf * HH + h
                    wait("s1_ps", 16, k + 1)
                    for t in range(TT):
                        ins = V_.tensor_reduce(mnegv[:, t, h:h + 1], ps(0, QSEG[t], (t + 1) * P), AX_X, ALU.max, negate=True)
                    ins.then_inc(s["smax_done"], 1)

                def max_parts(hf, g):
                    k = hf * 2 + g
                    wait("smax_done", 16, hf * HH + (g + 1) * GH)
                    src = mnegv[:, :, g * GH:(g + 1) * GH]
                    link(V_.tensor_scalar(mstv[:, :, :, 0], src, 2.0 ** -12, None, ALU.mult))
                    V_.scalar_tensor_tensor(out=mstv[:, :, :, 1], in0=src, scalar=2.0 ** -12, in1=mstv[:, :, :, 0], op0=ALU.mult, op1=ALU.subtract).then_inc(s["mst_done"], 1)
                    wait("mt_copied", 4, k + 1)
                    V_.tensor_copy(QT[ST:ST + MR, g * GH + 1:(g + 1) * GH, :],
                                   QT[ST:ST + MR, g * GH, :].unsqueeze(1).broadcast_to([MR, GH - 1, S])).then_inc(s["mrow_done"], 1)

                def p_lo(hf, h):
                    k = hf * HH + h
                    wait("phi_done", 16, k + 1)
                    V_.tensor_tensor(PLO[h % 2], P32[h % 2], PHI[h % 2], ALU.subtract).then_inc(s["plo_done"], 1)

                def y_norm(hf, g):
                    k = hf * 2 + g
                    wait("y_copied", 16, hf * HH + (g + 1) * GH)
                    link(V_.reciprocal(yrec[:, :].rearrange("p (h t) -> p h t", h=GH), Ysb[:, :, :, 2 * HD]))
                    if k:
                        wait("yt_ps", 4, k)
                    yv = Yf.rearrange("p t h c -> p h t c")
                    link(V_.tensor_tensor(yv, Ysb[:, :, :, 0:HD], Ysb[:, :, :, HD:2 * HD], ALU.add))
                    V_.tensor_tensor(yv, yv, yrec[:, :].rearrange("p (h t) -> p h t", h=GH).unsqueeze(3).broadcast_to([P, GH, TT, HD]), ALU.mult).then_inc(s["ynorm_done"], 1)

                def yt_lo(hf, g):
                    k = hf * 2 + g
                    wait("yt_hi", 4, k + 1)
                    V_.tensor_tensor(YT[:, 1, k, :], ps(7), YT[:, 0, k, :], ALU.subtract).then_inc(s["yt_lo"], 1)

                for hf in range(2):
                    tile_norms(hf, 0)
                    for t in range(TT):
                        if t + 1 < TT:
                            tile_norms(hf, t + 1)
                        stack_lo(hf, t)
                        kt_out(hf, t)
                    for h in range(GH):
                        row_max(hf, h)
                    max_parts(hf, 0)
                    for h in range(GH):
                        row_max(hf, GH + h)
                        p_lo(hf, h)
                    max_parts(hf, 1)
                    p_lo(hf, 4)
                    y_norm(hf, 0)
                    p_lo(hf, 5)
                    yt_lo(hf, 0)
                    p_lo(hf, 6)
                    p_lo(hf, 7)
                    y_norm(hf, 1)
                    yt_lo(hf, 1)

                for t in range(TT):
                    wait("op_ps", TT, t + 1)
                    link(V_.scalar_tensor_tensor(out=xres[:, t, :], in0=ps(t), scalar=unscale[:, 2:3], in1=xres[:, t, :], op0=ALU.mult, op1=ALU.add))
                    norm_stats(2, t, xres)
                    if t:
                        norm_out(2, t - 1, xres)
                norm_out(2, TT - 1, xres)
                xt_lo(2)
                ffn(1)
                for t in range(TT):
                    wait("acc_done", 8, TT + t + 1)
                    V_.scalar_tensor_tensor(out=xres[:, t, :], in0=ps(t), scalar=unscale[:, 0:1], in1=xres[:, t, :], op0=ALU.mult, op1=ALU.add).then_inc(s["out_ready"], 1)
                assert n[0] == LINKS, (n[0], LINKS)

        @block.tensor
        def _(pe):
            T_ = nc.tensor

            def three(o, lhs, rhs, first, last):
                T_.matmul(o, lhs(0), rhs(0), start=first, stop=False)
                T_.matmul(o, lhs(0), rhs(1), start=False, stop=False)
                return T_.matmul(o, lhs(1), rhs(0), start=False, stop=last)

            pe.wait_ge(s["c_made"], 1)
            for j in range(8):
                pe.wait_ge(s["wscaled"], j + 1)
                if j >= 2:
                    pe.wait_ge(s["w_lo"], 4 * (j - 1))
                for k in range(KC):
                    for i in range(4):
                        ins = T_.transpose(ps((j % 2) * 4 + k, i * P, P), RAW[j % 4][:, i, k * P:(k + 1) * P], ident[:, :])
                ins.then_inc(s["w_tr"], 1)
            pe.wait_ge(s["down_in"], 64)
            pe.wait_ge(s["w_lo"], 32)
            for m in range(16):
                q, t = m // 4, m % 4
                if m >= 8:
                    pe.wait_ge(s["dn_st"], m - 7)
                for i in range(4):
                    ins = T_.transpose(ps(m % 8, i * P, P), RAWD[t][:, (4 * q + i) * P:(4 * q + i + 1) * P], ident[:, :])
                ins.then_inc(s["dn_tr"], 1)
            pe.wait_ge(s["wd_lo"], 4)
            pe.wait_ge(s["pro_lo"], 2)
            pe.wait_ge(s["sel_done"], 1)

            with pe.Fori(0, B) as it:
                wait = per(pe, it)

                def transpose_x(u):
                    for t in range(TT):
                        wait("xn_done", 12, 4 * u + t + 1)
                        for k in range(KC):
                            ins = T_.transpose(ps(4 + k, t * P, P), xn[:, t, k * P:(k + 1) * P], ident[:, :])
                            if t == TT - 1:
                                ins.then_inc(s["xt_ps"], 1)
                    wait("xt_lo", 12, 4 * (u + 1))

                def ffn(f):
                    def gate_up(c):
                        k = f * HC + c
                        if c >= 2:
                            wait("gated", 32, k - 1)
                        for b, W, name in ((4, WG, "g_ps"), (5, WU, "u_ps")):
                            for kc in range(KC):
                                ins = three(ps(b + 2 * (c % 2)), lambda q: W[:, q, kc, c * P:(c + 1) * P], lambda q: XT[:, q, kc, :], kc == 0, kc == KC - 1)
                            ins.then_inc(s[name], 1)

                    def down(c):
                        wait("h_lo", 32, f * HC + c + 1)
                        parts = (Hhi[c % 2], Hlo[c % 2])
                        for t in range(TT):
                            ins = three(ps(t), lambda q: parts[q][:, t * P:(t + 1) * P], lambda q: WD[:, q, c, :], c == 0, c == HC - 1)
                            if c == HC - 1:
                                ins.then_inc(s["acc_done"], 1)
                            elif t == TT - 1:
                                ins.then_inc(s["down_done"], 1)

                    gate_up(0)
                    for c in range(HC):
                        if c + 1 < HC:
                            gate_up(c + 1)
                        down(c)

                def qkv(hf, t):
                    i, b2 = hf * TT + t, t % 2
                    if t >= 2:
                        wait("vlo_done", 8, i - 1)
                    for kc in range(KC):
                        ins = three(ps(2 * b2).rearrange("p (a n) -> p a n", a=2), lambda q: XT[:, q, kc, t * P:(t + 1) * P],
                                    lambda q: WQ[:, q, kc, 0:2 * D].rearrange("p (a n) -> p a n", a=2)[:, :, hf * 256:(hf + 1) * 256], kc == 0, kc == KC - 1)
                    ins.then_inc(s["qk_ps"], 1)
                    for kc in range(KC):
                        ins = three(ps(2 * b2 + 1, 0, 256), lambda q: XT[:, q, kc, t * P:(t + 1) * P],
                                    lambda q: WQ[:, q, kc, 2 * D + hf * 256:2 * D + (hf + 1) * 256], kc == 0, kc == KC - 1)
                    ins.then_inc(s["v_ps"], 1)

                def stacks(hf, t):
                    i, b2 = hf * TT + t, t % 2
                    wait("st_lo", 8, i + 1)
                    if t >= 2:
                        wait("qt_ev", 8, i - 1)
                        wait("kt_ev", 8, i - 1)
                    for b, a, name in ((4, 0, "qt_ps"), (5, HH, "kt_ps")):
                        for h in range(HH):
                            ins = T_.transpose(ps16(b + 2 * b2)[0:ST, h * P:(h + 1) * P], STK[b2][:, a + h, :], ident16[:, :])
                        ins.then_inc(s[name], 1)

                def scores_for_max(hf, h):
                    k = hf * HH + h
                    if h:
                        wait("smax_done", 16, k)
                    for t in (3, 2, 0, 1):
                        w = (t + 1) * P
                        T_.matmul(ps(0, QSEG[t], w), QT[0:ST, h, t * P:(t + 1) * P], KT[0:ST, h, 0:w], start=True, stop=False)
                        ins = T_.matmul(ps(0, QSEG[t] + t * P, P), identb[:, :], maskq[:, :], start=False, stop=True)
                    ins.then_inc(s["s1_ps"], 1)

                def transpose_max(hf, g):
                    k = hf * 2 + g
                    wait("mst_done", 4, k + 1)
                    for t in range(TT):
                        ins = T_.transpose(ps16(7)[ST:ST + MR, t * P:(t + 1) * P], mst[:, t * MR:(t + 1) * MR], ident16[:, :])
                    ins.then_inc(s["mt_ps"], 1)

                def scores(hf, h):
                    k = hf * HH + h
                    if h % GH == 0:
                        wait("mrow_done", 4, k // GH + 1)
                    if h:
                        wait("exp_done", 16, k)
                    for t in (0, 1, 3, 2):
                        w = (TT - t) * P
                        T_.matmul(ps(3, KSEG[t], w), KT[0:ST + MR, h, t * P:(t + 1) * P], QT[0:ST + MR, h, t * P:S], start=True, stop=False)
                        ins = T_.matmul(ps(3, KSEG[t], P), identb[:, :], maskk[:, :], start=False, stop=True)
                    ins.then_inc(s["s2_ps"], 1)

                def values(hf, h):
                    k = hf * HH + h
                    wait("plo_done", 16, k + 1)
                    if h:
                        wait("y_copied", 16, k)
                    for t in range(TT):
                        for kt in range(t + 1):
                            c = KSEG[kt] + (t - kt) * P
                            T_.matmul(ps(6, t * YW, YW), PHI[h % 2][:, c:c + P], V[:, kt, h, 0:YW], start=kt == 0, stop=False)
                            ins = T_.matmul(ps(6, t * YW + HD, HD + 1), PLO[h % 2][:, c:c + P], V[:, kt, h, HD:YW], start=False, stop=kt == t)
                    ins.then_inc(s["pv_ps"], 1)

                def transpose_y(hf, g):
                    k = hf * 2 + g
                    wait("ynorm_done", 4, k + 1)
                    if g:
                        wait("yt_lo", 4, k)
                    for t in range(TT):
                        ins = T_.transpose(ps(7, t * P, P), Yf[:, t].rearrange("p h c -> p (h c)"), ident[:, :])
                    ins.then_inc(s["yt_ps"], 1)

                transpose_x(0)
                ffn(0)
                transpose_x(1)
                for hf in range(2):
                    qkv(hf, 0)
                    for t in range(TT):
                        if t + 1 < TT:
                            qkv(hf, t + 1)
                        stacks(hf, t)
                    wait("qt_ev", 8, (hf + 1) * TT)
                    wait("kt_ev", 8, (hf + 1) * TT)
                    for h in range(GH):
                        scores_for_max(hf, h)
                    transpose_max(hf, 0)
                    for h in range(GH):
                        scores(hf, h)
                        scores_for_max(hf, GH + h)
                        if h:
                            values(hf, h - 1)
                    transpose_max(hf, 1)
                    for h in range(GH, HH):
                        scores(hf, h)
                        values(hf, h - 1)
                        if h == 5:
                            transpose_y(hf, 0)
                    values(hf, HH - 1)
                    transpose_y(hf, 1)
                wait("yt_lo", 4, 4)
                for t in range(TT):
                    for kc in range(KC):
                        ins = three(ps(t), lambda q: YT[:, q, kc, t * P:(t + 1) * P], lambda q: WO[:, q, kc, :], kc == 0, kc == KC - 1)
                    ins.then_inc(s["op_ps"], 1)
                transpose_x(2)
                ffn(1)


_INS = ["L0_attn_x", "L0_attn_w_qkv", "L0_attn_w_out", "L0_attn_q_gain", "L0_ffn_w_gate", "L0_ffn_w_up", "L0_ffn_w_down"]


def rope_table():
    import numpy as np
    half = HD // 2
    freq = np.float32(10000.0) ** (-np.arange(half, dtype=np.float32) / np.float32(half))
    theta = np.arange(S, dtype=np.float32)[:, None] * freq[None, :]
    c, sn = np.cos(theta), np.sin(theta)
    return np.concatenate([c, c, -sn, sn], axis=1).astype(np.float32)


def kernel(**inputs):
    import numpy as np
    import concourse.bacc as bacc
    from concourse.bass_utils import run_bass_kernel_spmd

    nc = bacc.Bacc("TRN2", target_bir_lowering=False, num_devices=1)
    arrays, args = {}, []
    for name in _INS:
        a = np.ascontiguousarray(inputs[name])
        arrays[f"in_{name}"] = a
        args.append(nc.dram_tensor(f"in_{name}", a.shape, F32, kind="ExternalInput").ap())
    arrays["rope_table"] = rope_table()
    args.append(nc.dram_tensor("rope_table", (S, 64), F32, kind="ExternalInput").ap())
    args.append(nc.dram_tensor("out", (B, S, D), F32, kind="ExternalOutput").ap())
    build(nc, *args)
    r = run_bass_kernel_spmd(nc, [arrays], core_ids=[0])
    return r.results[0]["out"]
```

```python
import concourse.bass as bass
from concourse import mybir
from concourse.alu_op_type import AluOpType as ALU

ACT = mybir.ActivationFunctionType
AX_X = mybir.AxisListType.X
RMAX = bass.bass_isa.ReduceOp.max
F32, F16, BF16, I32 = mybir.dt.float32, mybir.dt.float16, mybir.dt.bfloat16, mybir.dt.int32

P = 128
B, S, D, H = 8, 512, 512, 16
HD = D // H
HID = 2048
KC = D // P
TT = S // P
HC = HID // P
HH = H // 2
TH = S // 2
GH = 4
ST = 3 * HD
MR = 2 * GH
VW = 2 * HD + 2
YW = 2 * HD + 1
SW = P * TT * (TT + 1) // 2
LN_EPS, QK_EPS = 1e-5, 1e-6
LEAST = 2.0 ** -60
MASKED = -1e36
EXP_BITS = 0x7F800000
LN2 = 0.6931471805599453


def build(nc, x, w_qkv, w_out, q_gain, w_gate, w_up, w_down, rope, out):
    def sb(name, cols, dt):
        return nc.alloc_sbuf_tensor(name, [P, cols], dt)

    WG = sb("WG", 2 * KC * HID, F16)[:, :].rearrange("p (s k n) -> p s k n", s=2, k=KC)
    WU = sb("WU", 2 * KC * HID, F16)[:, :].rearrange("p (s k n) -> p s k n", s=2, k=KC)
    WD = sb("WD", 2 * HC * D, F16)[:, :].rearrange("p (s k n) -> p s k n", s=2, k=HC)
    WQ = sb("WQ", 2 * KC * 3 * D, F16)[:, :].rearrange("p (s k n) -> p s k n", s=2, k=KC)
    WO = sb("WO", 2 * KC * D, F16)[:, :].rearrange("p (s k n) -> p s k n", s=2, k=KC)

    at, place = 0, {}
    for name, words in (("xa", TT * D), ("xb", TT * D), ("xt", KC * S), ("qt", HH * S // 2),
                        ("kt", HH * S // 2), ("v", TT * HH * VW // 2), ("work", 3332), ("ffn", 2 * TH + 2 * TH),
                        ("xt2", KC * S), ("yt", S * 2), ("xn", D)):
        place[name] = (at, words)
        at += words
    arena = sb("arena", at, F32)

    def words(name, first=0, n=None):
        a, size = place[name]
        n = size - first if n is None else n
        assert first + n <= size
        return arena[:, a + first:a + first + n]

    def halves(name, first=0, n=None):
        return words(name, first, n).bitcast(F16)

    xa = words("xa").rearrange("p (t d) -> p t d", t=TT)
    xb = words("xb").rearrange("p (t d) -> p t d", t=TT)
    xn = words("xn")
    XT = [halves(n).rearrange("p (s k n) -> p s k n", s=2, k=KC) for n in ("xt", "xt2")]
    YT = [halves(n, 0, 2 * S).rearrange("p (s k n) -> p s k n", s=2, k=2) for n in ("yt", "xt")]
    QT = halves("qt").rearrange("p (h n) -> p h n", h=HH)
    KT = halves("kt").rearrange("p (h n) -> p h n", h=HH)
    V = halves("v").rearrange("p (t h c) -> p t h c", t=TT, h=HH)
    P32 = words("work", 0, SW)
    PHI = halves("work", SW, SW // 2)
    PLO = halves("work", SW + SW // 2, SW // 2)
    Yf = words("work", 2 * SW, TT * P).rearrange("p (t h c) -> p t h c", t=TT, h=GH)
    Ysb = words("work", 2 * SW + TT * P, TT * YW).rearrange("p (t c) -> p t c", t=TT)
    qs = [words("work", D * i, D) for i in range(2)]
    qn = [words("work", 2 * D + D * i, D) for i in range(2)]
    ropeU = words("work", 4 * D, D // 2)
    ropeV = words("work", 4 * D + D // 2, D // 2)
    STK = halves("work", 5 * D, HH * ST).rearrange("p (h c) -> p h c", h=2 * HH)
    fH = [words("ffn", TH * i, TH) for i in range(2)]
    HP = [[halves("ffn", 2 * TH + TH * q + TH // 2 * i, TH // 2) for q in range(2)] for i in range(2)]
    RAW = [arena[:, 2048 * (i + 1):2048 * (i + 2)].rearrange("p (i d) -> p i d", i=4) for i in range(4)]
    w0 = place["work"][0]
    RAWD = [arena[:, 0:2048]] + [arena[:, w0 + 2048 * i:w0 + 2048 * (i + 1)] for i in range(3)]
    WD32 = arena[:, 2048:2048 + HC * D]
    RAWQ = arena[:, w0:w0 + KC * 3 * D]
    RAWO = arena[:, 0:KC * D]

    ident = sb("ident", P, F32)
    ident16 = sb("ident16", P, F16)
    identb = sb("identb", P, BF16)
    maskq = sb("maskq", P, BF16)
    maskk = sb("maskk", P, BF16)
    ropet = sb("ropet", TT * 64, F32)
    ropev = ropet[:, :].rearrange("p (t c) -> p t c", t=TT)
    gain = sb("gain", 5 * H, F32)
    hscale = sb("hscale", H, F32)
    wmax = sb("wmax", 32, F32)
    wpow = sb("wpow", 32, F32)
    wrec = sb("wrec", 32, F32)
    wscale = sb("wscale", 32, F32)
    tscale = sb("tscale", HC, F32)
    pgu = sb("pgu", HC, F32)
    gmax = sb("gmax", 3, F32)
    gall = sb("gall", 3, F32)
    gpow = sb("gpow", 3, F32)
    grec = sb("grec", 3, F32)
    gscale = sb("gscale", 3, F32)
    unscale = sb("unscale", 4, F32)
    stat = sb("stat", 6 * TT, F32)
    mv = sb("mv", 2 * TT, F32)
    var2 = sb("var2", TT, F32)
    rstd = sb("rstd", TT, F32)
    mhalf = sb("mhalf", 2 * HH, F32)
    ss = sb("ss", 4 * HH, F32)
    ss2 = sb("ss2", 4 * HH, F32)
    rn = sb("rn", 4 * HH, F32)
    mneg = sb("mneg", TT * HH, F32)
    mst = sb("mst", TT * MR, F16)
    yrec = sb("yrec", GH * TT, F32)
    carrier = sb("carrier", 3 * TT, F32)
    lnbias = sb("lnbias", 1, F32)

    psum = nc.alloc_psum_tensor("psum", [P, 8 * 512], F32)

    def ps(b, a=0, n=512):
        return psum[:, b * 512 + a:b * 512 + a + n]

    def ps16(b):
        return psum[:, b * 512:(b + 1) * 512].bitcast(F16)

    QSEG = {3: 0, 2: 512, 0: 896, 1: 1024}
    KSEG = {0: 0, 1: 512, 3: 896, 2: 1024}

    names = """c_in raw0 raw1 raw2 raw3 down_in qkv_in out_in c_made wscaled wsent w_tr w_hi w_lo
        dn_tr dn_st gmax_in gmax_all scales wd_hi wd_lo sel_done pro_hi pro_lo dve_pro pool_pro
        x_loaded x_stored x1_done x2_done out_ready var_ready rstd_ready xn_done xt_ps xt_hi xt_lo
        qk_ps v_ps qs_done sq_done vhi_done vlo_done ssq_ready r_ready qn_done rope_done
        st_hi st_lo qt_ps kt_ps qt_ev kt_ev s1_ps smax_done mst_done mt_ps mt_copied mrow_done
        s2_ps exp_done phi_done plo_done pv_ps y_copied ynorm_done yt_ps yt_hi yt_lo op_ps
        dve_chain pool_chain"""
    ffn_names = "gu_ps tanh_done a_done gated h_hi h_lo down_done"
    names = names.split() + [f"{n}{f}" for n in ffn_names.split() for f in range(2)]
    s = {n: nc.alloc_semaphore(n) for n in names}

    def per(eng, it, ahead):
        def wait(name, n, k, batch=0):
            eng.wait_ge(s[name], it * n + (ahead + batch) * n + k)
        return wait

    def ffn_point(f, i, first, end):
        o = []
        if i - 2 >= first:
            o.append(("down", f, i - 2))
        if i < end:
            o += [("gate", f, i), ("up", f, i)]
        if first <= i - 1 < end:
            o += [("gated", f, i - 1), ("parts", f, i - 1)]
        if i - 2 >= first and (i - 2) % HC == HC - 1:
            o.append(("residual", f, (i - 2) // HC))
        return o

    STEPS = 2 * HC
    AHEAD = 4

    def order(fill):
        o = []
        if fill is None:
            for i in range(STEPS + 2):
                o += ffn_point(1, i, 0, STEPS)
            return o
        points = [ffn_point(1, i, AHEAD, STEPS) for i in range(AHEAD, STEPS + 2)] if fill else []

        def some():
            if points:
                o.extend(points.pop(0))

        early = [ffn_point(1, i, 0, AHEAD) for i in range(AHEAD + 2)] if fill else [[]] * (AHEAD + 2)
        o += early[0] + early[1] + early[2]
        o += [("stats", 0, 0), ("stats", 0, 1)] + early[3]
        o += [("norm", 0, 0)] + early[4] + [("split", 0, 0), ("norm", 0, 1)] + early[5] + [("split", 0, 1)]
        late = {0: [("stats", 0, 2), ("norm", 0, 2)], 1: [("split", 0, 2), ("stats", 0, 3)], 2: [("norm", 0, 3)],
                3: [("split", 0, 3)],
                HC + 2: [("stats", 1, 0)], HC + 3: [("norm", 1, 0), ("stats", 1, 1)], HC + 4: [("split", 1, 0)],
                HC + 5: [("norm", 1, 1)], HC + 6: [("split", 1, 1)]}
        for i in range(STEPS + 2):
            o += ffn_point(0, i, 0, STEPS) + late.get(i, [])
        rest = [[("stats", 1, 2), ("stats", 1, 3), ("norm", 1, 2), ("split", 1, 2), ("norm", 1, 3)], [("split", 1, 3)]]
        for hf in range(2):
            for t in range(TT + 1):
                if t < TT:
                    o.append(("qkv", hf, t))
                if t:
                    o.append(("unit", hf, t - 1))
                if hf == 0 and t < 2:
                    o += rest[t]
                if t < TT:
                    o.append(("qkv out", hf, t))
                some()
                if t:
                    o += [("stack", hf, t - 1), ("stack out", hf, t - 1)]
            for h in range(GH):
                o += [("scores max", hf, h), ("row max", hf, h)]
                if h % 2:
                    some()
            o.append(("max rows", hf, 0))
            for h in range(HH):
                o.append(("scores", hf, h))
                if h:
                    o.append(("values", hf, h - 1))
                some()
                o.append(("exp", hf, h))
                if h < GH:
                    o += [("scores max", hf, GH + h), ("row max", hf, GH + h)]
                if h:
                    o.append(("y out", hf, h - 1))
                if h == GH - 1:
                    o.append(("max rows", hf, 1))
                if h == GH:
                    o.append(("y turn", hf, 0))
            o += [("values", hf, HH - 1), ("y out", hf, HH - 1)]
            if hf == 0:
                some()
            o.append(("y turn", hf, 1))
        while points:
            some()
        for t in range(TT + 2):
            if t < TT:
                o.append(("out", 0, t))
            if 0 < t <= TT:
                o.append(("norm", 2, t - 1))
            if t < TT:
                o += [("out residual", 0, t), ("stats", 2, t)]
            if t > 1:
                o.append(("split", 2, t - 2))
        return o

    def run(stages, fill):
        for name, a, b in order(fill):
            if name in stages:
                stages[name](a, b)

    with nc.Block() as block:

        @block.sync
        def _(sp):
            sp.dma_start(ropev, rope.rearrange("(t p) c -> p t c", p=P)).then_inc(s["c_in"], 16)
            sp.dma_start(gain[:, 0:H], q_gain.rearrange("(a n) -> a n", a=1).broadcast_to([P, H])).then_inc(s["c_in"], 16)
            for j in range(8):
                w = (w_gate if j < 4 else w_up)[(j % 4) * 512:(j % 4 + 1) * 512, :]
                if j >= 4:
                    sp.wait_ge(s["w_tr"], j - 3)
                sp.dma_start(RAW[j % 4], w.rearrange("(i p) d -> p i d", p=P)).then_inc(s[f"raw{j % 4}"], 16)
                if j == 3:
                    for t in range(4):
                        sp.dma_start(RAWD[t], w_down[t * P:(t + 1) * P, :]).then_inc(s["down_in"], 16)
            sp.wait_ge(s["dn_tr"], 16)
            sp.dma_start(RAWQ.rearrange("p (k n) -> p k n", k=KC), w_qkv.rearrange("(k p) n -> p k n", p=P)).then_inc(s["qkv_in"], 16)
            sp.dma_start(RAWO.rearrange("p (k n) -> p k n", k=KC), w_out.rearrange("(k p) n -> p k n", p=P)).then_inc(s["out_in"], 16)
            sp.wait_ge(s["pro_lo"], 2)
            sp.dma_start(xa, x[0].rearrange("(t p) d -> p t d", p=P)).then_inc(s["x_loaded"], 16)
            with sp.Fori(0, B - 1) as it:
                sp.wait_ge(s["x2_done"], it * TT + TT)
                sp.dma_start(xa, x[it + 1].rearrange("(t p) d -> p t d", p=P)).then_inc(s["x_loaded"], 16)
                sp.wait_ge(s["out_ready"], it * TT + TT)
                sp.dma_start(out[it].rearrange("(t p) d -> p t d", p=P), xb).then_inc(s["x_stored"], 16)
            sp.wait_ge(s["out_ready"], B * TT)
            sp.dma_start(out[B - 1].rearrange("(t p) d -> p t d", p=P), xb).then_inc(s["x_stored"], 16)
            sp.wait_ge(s["x_stored"], 16 * B)

        @block.gpsimd
        def _(pool):
            n = [0]

            def link(ins):
                n[0] += 1
                ins.then_inc(s["pool_pro"], 1)
                pool.wait_ge(s["pool_pro"], n[0])

            for m in (ident, ident16, identb, maskq, maskk):
                link(nc.gpsimd.memset(m[:, :], 0.0))
            link(nc.gpsimd.memset(mhalf[:, :], -0.5))
            link(nc.gpsimd.memset(mst[:, :], 0.0))
            link(nc.gpsimd.memset(halves("v"), 1.0))
            for m in (ident, ident16, identb):
                link(nc.gpsimd.affine_select(out=m[:, :], in_=m[:, :], compare_op=ALU.not_equal, fill=1.0,
                                             base=0, pattern=[[-1, P]], channel_multiplier=1))
            link(nc.gpsimd.affine_select(out=maskq[:, :], in_=maskq[:, :], compare_op=ALU.is_ge, fill=MASKED,
                                         base=0, pattern=[[-1, P]], channel_multiplier=1))
            nc.gpsimd.affine_select(out=maskk[:, :], in_=maskk[:, :], compare_op=ALU.is_ge, fill=MASKED,
                                    base=0, pattern=[[1, P]], channel_multiplier=-1).then_inc(s["c_made"], 1)
            pool.wait_ge(s["gmax_in"], 3)
            nc.gpsimd.partition_all_reduce(gall[:, :], gmax[:, :], P, RMAX).then_inc(s["gmax_all"], 1)
            pool.wait_ge(s["wd_lo"], 4)
            kr = KT[ST:ST + MR, :, :]
            link(nc.gpsimd.memset(kr, 4096.0))
            krv = KT[ST:ST + MR, :, :].rearrange("p (a g) n -> p a g n", g=GH)
            link(nc.gpsimd.affine_select(out=krv, in_=krv, compare_op=ALU.is_ge, fill=0.0, base=0,
                                         pattern=[[0, 2], [-2, GH], [0, S]], channel_multiplier=1))
            nc.gpsimd.affine_select(out=krv, in_=krv, compare_op=ALU.is_ge, fill=0.0, base=1,
                                    pattern=[[0, 2], [2, GH], [0, S]], channel_multiplier=-1).then_inc(s["sel_done"], 1)
            pool.wait_ge(s["sel_done"], 1)

            def batch(it, ahead, fill):
                wait = per(pool, it, ahead)
                turns = [0]

                def stats(u, t):
                    wait("var_ready", 12, 4 * u + t + 1)
                    nc.gpsimd.tensor_tensor(rstd[:, t:t + 1], var2[:, t:t + 1], mhalf[:, 0:1], ALU.pow).then_inc(s["rstd_ready"], 1)

                def qkv_out(hf, t):
                    i, c = hf * TT + t, slice(16 * (t % 2), 16 * (t % 2) + 16)
                    wait("ssq_ready", 8, i + 1)
                    nc.gpsimd.tensor_tensor(rn[:, c], ss2[:, c], mhalf[:, :], ALU.pow).then_inc(s["r_ready"], 1)

                def rotate(hf, t):
                    i = hf * TT + t
                    wait("qn_done", 8, i + 1)
                    ev = qn[t % 2].rearrange("p (e o c) -> p e o c", o=2, c=HD)[:, :, 0, :]
                    U = ropeU.rearrange("p (e c) -> p e c", c=HD)
                    W = ropeV.rearrange("p (e c) -> p e c", c=HD)
                    hw = HD // 2

                    def table(a, w):
                        return ropev[:, t, a:a + w].unsqueeze(1).broadcast_to([P, HH, w])

                    nc.gpsimd.tensor_tensor(U, ev, table(0, HD), ALU.mult)
                    nc.gpsimd.tensor_tensor(W[:, :, 0:hw], ev[:, :, hw:HD], table(HD, hw), ALU.mult)
                    turns[0] += 1
                    nc.gpsimd.tensor_tensor(W[:, :, hw:HD], ev[:, :, 0:hw], table(HD + hw, hw), ALU.mult).then_inc(s["pool_chain"], 1)
                    wait("pool_chain", 8, turns[0])
                    nc.gpsimd.tensor_tensor(ev, U, W, ALU.add).then_inc(s["rope_done"], 1)

                run({"stats": stats, "qkv out": qkv_out, "unit": rotate}, fill)

            batch(0, 0, False)
            with pool.Fori(0, B - 1) as it:
                batch(it, 1, True)

        @block.scalar
        def _(act):
            for j in range(8):
                r = RAW[j % 4]
                act.wait_ge(s["wsent"], j + 1)
                for i in range(4):
                    c = 4 * j + i
                    ins = nc.scalar.activation(r[:, i, :], r[:, i, :], ACT.Copy, scale=wscale[:, c:c + 1])
                ins.then_inc(s["wscaled"], 1)
                act.wait_ge(s["w_tr"], j + 1)
                W = WG if j < 4 else WU
                for k in range(KC):
                    nc.scalar.activation(W[:, 0, k, (j % 4) * 512:(j % 4 + 1) * 512], ps((j % 2) * 4 + k), ACT.Copy).then_inc(s["w_hi"], 1)
            act.wait_ge(s["scales"], 1)
            for q in range(4):
                nc.scalar.activation(WD[:, 0, 4 * q:4 * q + 4, :], WD32[:, 2048 * q:2048 * (q + 1)].rearrange("p (k n) -> p k n", n=D),
                                     ACT.Copy, scale=gscale[:, 0:1]).then_inc(s["wd_hi"], 1)
            nc.scalar.activation(WQ[:, 0], RAWQ.rearrange("p (k n) -> p k n", k=KC), ACT.Copy, scale=gscale[:, 1:2]).then_inc(s["pro_hi"], 1)
            nc.scalar.activation(WO[:, 0], RAWO.rearrange("p (k n) -> p k n", k=KC), ACT.Copy, scale=gscale[:, 2:3]).then_inc(s["pro_hi"], 1)

            def batch(it, ahead, fill):
                wait = per(act, it, ahead)

                def split(u, t):
                    wait("xt_ps", 12, 4 * u + t + 1)
                    nc.scalar.activation(XT[u // 2][:, 0, :, t * P:(t + 1) * P], ps(3).rearrange("p (k n) -> p k n", k=KC), ACT.Copy).then_inc(s["xt_hi"], 1)

                def qkv_out(hf, t):
                    i, b2 = hf * TT + t, t % 2
                    wait("qk_ps", 8, i + 1)
                    if t >= 2:
                        wait("st_lo", 8, i - 1)
                    nc.scalar.activation(qs[b2], ps(0), ACT.Copy, scale=unscale[:, 1:2]).then_inc(s["qs_done"], 1)
                    nc.scalar.activation(qn[b2], ps(0), ACT.Square, scale=unscale[:, 1:2]).then_inc(s["sq_done"], 1)
                    wait("v_ps", 8, i + 1)
                    nc.scalar.activation(V[:, t, :, HD:2 * HD], ps(1, 0, 256).rearrange("p (h c) -> p h c", c=HD),
                                         ACT.Copy, scale=2.0 ** -17).then_inc(s["vhi_done"], 1)

                def stack(hf, t):
                    i = hf * TT + t
                    wait("rope_done", 8, i + 1)
                    if t:
                        wait("kt_ps", 8, i)
                    q3 = qn[t % 2].rearrange("p (h c) -> p h c", c=HD)
                    nc.scalar.activation(STK[:, :, 0:HD], q3, ACT.Copy)
                    nc.scalar.activation(STK[:, 0:HH, HD:2 * HD], q3[:, 0:HH, :], ACT.Copy)
                    nc.scalar.activation(STK[:, HH:2 * HH, 2 * HD:ST], q3[:, HH:2 * HH, :], ACT.Copy).then_inc(s["st_hi"], 1)

                def stack_out(hf, t):
                    wait("qt_ps", 8, hf * TT + t + 1)
                    nc.scalar.activation(QT[0:ST, :, t * P:(t + 1) * P], ps16(2)[0:ST, :].rearrange("p (h n) -> p h n", h=HH),
                                         ACT.Copy).then_inc(s["qt_ev"], 1)

                def max_rows(hf, g):
                    wait("mt_ps", 4, hf * 2 + g + 1)
                    nc.scalar.activation(QT[ST:ST + MR, g * GH, :], ps16(3)[ST:ST + MR, 0:S], ACT.Copy).then_inc(s["mt_copied"], 1)

                def exp(hf, h):
                    k = hf * HH + h
                    wait("s2_ps", 16, k + 1)
                    if k:
                        wait("plo_done", 16, k)
                    nc.scalar.activation(P32, ps(0, 0, SW), ACT.Exp, bias=lnbias[:, 0:1],
                                         scale=hscale[:, k:k + 1]).then_inc(s["exp_done"], 1)
                    if k:
                        wait("pv_ps", 16, k)
                    nc.scalar.activation(PHI, ps(0, 0, SW), ACT.Exp, bias=lnbias[:, 0:1],
                                         scale=hscale[:, k:k + 1]).then_inc(s["phi_done"], 1)

                def y_out(hf, h):
                    k = hf * HH + h
                    wait("pv_ps", 16, k + 1)
                    if k:
                        wait("ynorm_done", 16, k)
                    nc.scalar.activation(Ysb, ps(3, 0, TT * YW).rearrange("p (t c) -> p t c", t=TT), ACT.Copy).then_inc(s["y_copied"], 1)

                def y_turn(hf, g):
                    k = hf * 2 + g
                    wait("yt_ps", 4, k + 1)
                    nc.scalar.activation(YT[hf][:, 0, g, :], ps(3), ACT.Copy).then_inc(s["yt_hi"], 1)

                def gated(f, i):
                    wait(f"gu_ps{f}", 32, i + 1, -f)
                    if i >= 2:
                        wait(f"h_lo{f}", 32, i - 1, -f)
                    nc.scalar.activation(fH[i % 2], ps(4 + i % 2, 0, TH), ACT.Tanh, scale=tscale[:, i % HC:i % HC + 1]).then_inc(s[f"tanh_done{f}"], 1)

                def parts(f, i):
                    wait(f"gated{f}", 32, i + 1, -f)
                    if i >= 2:
                        wait(f"down_done{f}", 32, i - 1, -f)
                    nc.scalar.activation(HP[i % 2][0], fH[i % 2], ACT.Copy).then_inc(s[f"h_hi{f}"], 1)

                run({"split": split, "qkv out": qkv_out, "stack": stack, "stack out": stack_out, "max rows": max_rows,
                     "exp": exp, "y out": y_out, "y turn": y_turn, "gated": gated, "parts": parts}, fill)

            batch(0, 0, False)
            with act.Fori(0, B - 1) as it:
                batch(it, 1, True)
            batch(0, B, None)

        @block.vector
        def _(dve):
            V_ = nc.vector
            n = [0]

            def link(ins):
                n[0] += 1
                ins.then_inc(s["dve_pro"], 1)
                dve.wait_ge(s["dve_pro"], n[0])

            def power_of_two(out, in_):
                link(V_.tensor_scalar(out, in_, LEAST, None, ALU.max))
                link(V_.tensor_scalar(out.bitcast(I32), out.bitcast(I32), EXP_BITS, None, ALU.bitwise_and))

            link(V_.memset(lnbias[:, :], 14 * LN2))
            dve.wait_ge(s["c_in"], 32)
            g0, g1, g2, g3, g4 = (gain[:, i * H:(i + 1) * H] for i in range(5))
            link(V_.tensor_scalar(g1.bitcast(I32), g0.bitcast(I32), 0x7FFFFFFF, None, ALU.bitwise_and))
            power_of_two(g2, g1)
            link(V_.reciprocal(g3, g2))
            link(V_.tensor_tensor(g4, g0, g3, ALU.mult))
            link(V_.tensor_scalar(hscale[:, :], g2, 2.0 ** -24, None, ALU.mult))

            def w_scales(j):
                c = slice(4 * j, 4 * j + 4)
                dve.wait_ge(s[f"raw{j % 4}"], 16 * (j // 4 + 1))
                link(V_.tensor_reduce(wmax[:, c], RAW[j % 4], AX_X, ALU.max, apply_absolute_value=True))
                power_of_two(wpow[:, c], wmax[:, c])
                link(V_.reciprocal(wrec[:, c], wpow[:, c]))
                V_.tensor_scalar(wscale[:, c], wrec[:, c], 2.0 ** 13, None, ALU.mult).then_inc(s["wsent"], 1)

            w_scales(0)
            for j in range(8):
                if j + 1 < 8:
                    w_scales(j + 1)
                W = WG if j < 4 else WU
                for k in range(KC):
                    dve.wait_ge(s["w_hi"], 4 * j + k + 1)
                    c = slice((j % 4) * 512, (j % 4 + 1) * 512)
                    V_.tensor_tensor(W[:, 1, k, c], ps((j % 2) * 4 + k), W[:, 0, k, c], ALU.subtract).then_inc(s["w_lo"], 1)
            link(V_.tensor_scalar(tscale[:, :], wpow[:, 0:HC], 2.0 ** -23, None, ALU.mult))
            link(V_.scalar_tensor_tensor(out=pgu[:, :], in0=wpow[:, 0:HC], scalar=2.0 ** 5, in1=wpow[:, HC:2 * HC], op0=ALU.mult, op1=ALU.mult))
            WD32v = WD32.rearrange("p (k n) -> p k n", n=D)
            for m in range(16):
                q, t = m // 4, m % 4
                dve.wait_ge(s["dn_tr"], m + 1)
                ins = V_.tensor_tensor(WD32v[:, 4 * q:4 * q + 4, t * P:(t + 1) * P], ps(m % 8).rearrange("p (k n) -> p k n", n=P),
                                       pgu[:, 4 * q:4 * q + 4].unsqueeze(2).broadcast_to([P, 4, P]), ALU.mult)
                ins.then_inc(s["dn_st"], 1)
            dve.wait_ge(s["dn_st"], 16)
            V_.tensor_reduce(gmax[:, 0:1], WD32, AX_X, ALU.max, apply_absolute_value=True).then_inc(s["gmax_in"], 1)
            dve.wait_ge(s["qkv_in"], 16)
            V_.tensor_reduce(gmax[:, 1:2], RAWQ, AX_X, ALU.max, apply_absolute_value=True).then_inc(s["gmax_in"], 1)
            dve.wait_ge(s["out_in"], 16)
            V_.tensor_reduce(gmax[:, 2:3], RAWO, AX_X, ALU.max, apply_absolute_value=True).then_inc(s["gmax_in"], 1)
            dve.wait_ge(s["gmax_all"], 1)
            power_of_two(gpow[:, :], gall[:, :])
            link(V_.reciprocal(grec[:, :], gpow[:, :]))
            link(V_.tensor_scalar(unscale[:, 0:1], gpow[:, 0:1], 2.0 ** -14, None, ALU.mult))
            link(V_.tensor_scalar(unscale[:, 1:2], gpow[:, 1:2], 2.0 ** -22, None, ALU.mult))
            link(V_.scalar_tensor_tensor(out=unscale[:, 2:3], in0=gpow[:, 1:2], scalar=2.0 ** -18, in1=gpow[:, 2:3], op0=ALU.mult, op1=ALU.mult))
            V_.tensor_scalar(gscale[:, :], grec[:, :], 2.0 ** 13, None, ALU.mult).then_inc(s["scales"], 1)
            dve.wait_ge(s["scales"], 1)
            for q in range(4):
                dve.wait_ge(s["wd_hi"], q + 1)
                V_.scalar_tensor_tensor(out=WD[:, 1, 4 * q:4 * q + 4, :].rearrange("p k n -> p (k n)"), in0=WD32[:, 2048 * q:2048 * (q + 1)], scalar=gscale[:, 0:1],
                                        in1=WD[:, 0, 4 * q:4 * q + 4, :].rearrange("p k n -> p (k n)"), op0=ALU.mult, op1=ALU.subtract).then_inc(s["wd_lo"], 1)
            for W, raw, c, m in ((WQ, RAWQ, 1, 1), (WO, RAWO, 2, 2)):
                dve.wait_ge(s["pro_hi"], m)
                V_.scalar_tensor_tensor(out=W[:, 1].rearrange("p k n -> p (k n)"), in0=raw, scalar=gscale[:, c:c + 1],
                                        in1=W[:, 0].rearrange("p k n -> p (k n)"), op0=ALU.mult, op1=ALU.subtract).then_inc(s["pro_lo"], 1)

            LINKS = 3 * TT * 2 + 2 * TT * 2 + 4 + H * 2

            def batch(it, ahead, fill):
                wait = per(dve, it, ahead)
                n = [0]

                def link(ins):
                    n[0] += 1
                    ins.then_inc(s["dve_chain"], 1)
                    wait("dve_chain", LINKS, n[0])

                def stats(u, t):
                    src = (xa, xa, xb)[u]
                    if u == 0:
                        wait("x_loaded", 16, 16)
                    else:
                        wait(f"x{u}_done", TT, t + 1)
                    n[0] += 1
                    V_.bn_stats(stat[:, 6 * t:6 * t + 6], src[:, t, :]).then_inc(s["dve_chain"], 1)
                    wait("dve_chain", LINKS, n[0])
                    V_.memset(carrier[:, 4 * u + t:4 * u + t + 1], 0.0)
                    link(V_.bn_aggr(mv[:, 2 * t:2 * t + 2], stat[:, 6 * t:6 * t + 6]))
                    V_.tensor_scalar(var2[:, t:t + 1], mv[:, 2 * t + 1:2 * t + 2], LN_EPS, 2.0 ** -18, ALU.add, ALU.mult).then_inc(s["var_ready"], 1)

                def norm(u, t):
                    src = (xa, xa, xb)[u]
                    k = 4 * u + t
                    wait("rstd_ready", 12, k + 1)
                    if k:
                        wait("xt_ps", 12, k)
                    elif fill:
                        wait("xt_ps", 12, 12, -1)
                    V_.tensor_scalar(xn, src[:, t, :], mv[:, 2 * t:2 * t + 1], rstd[:, t:t + 1], ALU.subtract, ALU.mult).then_inc(s["xn_done"], 1)

                def split(u, t):
                    wait("xt_hi", 12, 4 * u + t + 1)
                    c = slice(t * P, (t + 1) * P)
                    V_.tensor_tensor(XT[u // 2][:, 1, :, c], ps(3).rearrange("p (k n) -> p k n", k=KC), XT[u // 2][:, 0, :, c], ALU.subtract).then_inc(s["xt_lo"], 1)

                def gated(f, i):
                    g, u = ps(4 + i % 2, 0, TH), ps(4 + i % 2, TH, TH)
                    wait(f"tanh_done{f}", 32, i + 1, -f)
                    V_.scalar_tensor_tensor(out=fH[i % 2], in0=fH[i % 2], scalar=1.0, in1=g, op0=ALU.add, op1=ALU.mult).then_inc(s[f"a_done{f}"], 1)
                    wait(f"a_done{f}", 32, i + 1, -f)
                    V_.scalar_tensor_tensor(out=fH[i % 2], in0=fH[i % 2], scalar=2.0 ** -50, in1=u, op0=ALU.mult, op1=ALU.mult).then_inc(s[f"gated{f}"], 1)

                def parts(f, i):
                    wait(f"h_hi{f}", 32, i + 1, -f)
                    V_.tensor_tensor(HP[i % 2][1], fH[i % 2], HP[i % 2][0], ALU.subtract).then_inc(s[f"h_lo{f}"], 1)

                def residual(f, th):
                    wait(f"down_done{f}", 32, HC * (th + 1), -f)
                    dst, name = ((xa, "x1_done"), (xb, "out_ready"))[f]
                    for t in (2 * th, 2 * th + 1):
                        V_.scalar_tensor_tensor(out=dst[:, t, :], in0=ps(6 * f + t % 2), scalar=unscale[:, 0:1], in1=dst[:, t, :],
                                                op0=ALU.mult, op1=ALU.add).then_inc(s[name], 1)

                def qkv_out(hf, t):
                    i, c = hf * TT + t, slice(16 * (t % 2), 16 * (t % 2) + 16)
                    wait("sq_done", 8, i + 1)
                    link(V_.tensor_reduce(ss[:, c], qn[t % 2].rearrange("p (h c) -> p h c", c=HD), AX_X, ALU.add))
                    V_.tensor_scalar(ss2[:, c], ss[:, c], QK_EPS, 2.0 ** -24, ALU.add, ALU.mult).then_inc(s["ssq_ready"], 1)
                    wait("vhi_done", 8, i + 1)
                    V_.scalar_tensor_tensor(out=V[:, t, :, 0:HD], in0=ps(1, 0, 256).rearrange("p (h c) -> p h c", c=HD), scalar=2.0 ** -17,
                                            in1=V[:, t, :, HD:2 * HD], op0=ALU.mult, op1=ALU.subtract).then_inc(s["vlo_done"], 1)

                def unit(hf, t):
                    i, b2 = hf * TT + t, t % 2
                    wait("r_ready", 8, i + 1)
                    link(V_.tensor_tensor(rn[:, 16 * b2:16 * b2 + HH], rn[:, 16 * b2:16 * b2 + HH], gain[:, 4 * H + hf * HH:4 * H + (hf + 1) * HH], ALU.mult))
                    V_.tensor_tensor(qn[b2].rearrange("p (h c) -> p h c", c=HD), qs[b2].rearrange("p (h c) -> p h c", c=HD),
                                     rn[:, 16 * b2:16 * b2 + 16].unsqueeze(2).broadcast_to([P, 2 * HH, HD]), ALU.mult).then_inc(s["qn_done"], 1)

                def stack(hf, t):
                    wait("st_hi", 8, hf * TT + t + 1)
                    q3 = qn[t % 2].rearrange("p (h c) -> p h c", c=HD)
                    V_.tensor_tensor(STK[:, 0:HH, 2 * HD:ST], q3[:, 0:HH, :], STK[:, 0:HH, 0:HD], ALU.subtract)
                    V_.tensor_tensor(STK[:, HH:2 * HH, HD:2 * HD], q3[:, HH:2 * HH, :], STK[:, HH:2 * HH, 0:HD], ALU.subtract).then_inc(s["st_lo"], 1)

                def stack_out(hf, t):
                    wait("kt_ps", 8, hf * TT + t + 1)
                    V_.tensor_copy(KT[0:ST, :, t * P:(t + 1) * P], ps16(3)[0:ST, :].rearrange("p (h n) -> p h n", h=HH)).then_inc(s["kt_ev"], 1)

                mnegv = mneg[:, :].rearrange("p (t h) -> p t h", t=TT)
                mstv = mst[:, :].rearrange("p (t h c) -> p t h c", t=TT, c=2)

                def row_max(hf, h):
                    wait("s1_ps", 16, hf * HH + h + 1)
                    for t in range(TT):
                        ins = V_.tensor_reduce(mnegv[:, t, h:h + 1], ps(0, QSEG[t], (t + 1) * P), AX_X, ALU.max, negate=True)
                    ins.then_inc(s["smax_done"], 1)

                def max_rows(hf, g):
                    k = hf * 2 + g
                    wait("smax_done", 16, hf * HH + (g + 1) * GH)
                    if k:
                        wait("mt_ps", 4, k)
                    src = mnegv[:, :, g * GH:(g + 1) * GH]
                    link(V_.tensor_scalar(mstv[:, :, :, 0], src, 2.0 ** -12, None, ALU.mult))
                    V_.scalar_tensor_tensor(out=mstv[:, :, :, 1], in0=src, scalar=2.0 ** -12, in1=mstv[:, :, :, 0], op0=ALU.mult, op1=ALU.subtract).then_inc(s["mst_done"], 1)
                    wait("mt_copied", 4, k + 1)
                    V_.tensor_copy(QT[ST:ST + MR, g * GH + 1:(g + 1) * GH, :],
                                   QT[ST:ST + MR, g * GH, :].unsqueeze(1).broadcast_to([MR, GH - 1, S])).then_inc(s["mrow_done"], 1)

                def exp(hf, h):
                    wait("phi_done", 16, hf * HH + h + 1)
                    V_.tensor_tensor(PLO, P32, PHI, ALU.subtract).then_inc(s["plo_done"], 1)

                def y_out(hf, h):
                    wait("y_copied", 16, hf * HH + h + 1)
                    if h % GH == 0 and hf * HH + h:
                        wait("yt_ps", 4, (hf * HH + h) // GH)
                    yv = Yf[:, :, h % GH, :]
                    link(V_.reciprocal(yrec[:, 0:TT], Ysb[:, :, 2 * HD]))
                    link(V_.tensor_tensor(yv, Ysb[:, :, 0:HD], Ysb[:, :, HD:2 * HD], ALU.add))
                    V_.tensor_tensor(yv, yv, yrec[:, 0:TT].unsqueeze(2).broadcast_to([P, TT, HD]), ALU.mult).then_inc(s["ynorm_done"], 1)

                def y_turn(hf, g):
                    wait("yt_hi", 4, hf * 2 + g + 1)
                    V_.tensor_tensor(YT[hf][:, 1, g, :], ps(3), YT[hf][:, 0, g, :], ALU.subtract).then_inc(s["yt_lo"], 1)

                def out_residual(_, t):
                    wait("op_ps", TT, t + 1)
                    if t == 0 and fill:
                        wait("x_stored", 16, 16, -1)
                    V_.scalar_tensor_tensor(out=xb[:, t, :], in0=ps(t % 3), scalar=unscale[:, 2:3], in1=xa[:, t, :], op0=ALU.mult, op1=ALU.add).then_inc(s["x2_done"], 1)

                run({"stats": stats, "norm": norm, "split": split, "gated": gated, "parts": parts, "residual": residual,
                     "qkv out": qkv_out, "unit": unit, "stack": stack, "stack out": stack_out, "row max": row_max,
                     "max rows": max_rows, "exp": exp, "y out": y_out, "y turn": y_turn, "out residual": out_residual}, fill)
                assert fill is None or n[0] == LINKS, (n[0], LINKS)

            batch(0, 0, False)
            with dve.Fori(0, B - 1) as it:
                batch(it, 1, True)
            batch(0, B, None)

        @block.tensor
        def _(pe):
            T_ = nc.tensor

            def three(o, lhs, rhs, first, last):
                T_.matmul(o, lhs(0), rhs(0), start=first, stop=False)
                T_.matmul(o, lhs(0), rhs(1), start=False, stop=False)
                return T_.matmul(o, lhs(1), rhs(0), start=False, stop=last)

            pe.wait_ge(s["c_made"], 1)
            for j in range(8):
                pe.wait_ge(s["wscaled"], j + 1)
                if j >= 2:
                    pe.wait_ge(s["w_lo"], 4 * (j - 1))
                for k in range(KC):
                    for i in range(4):
                        ins = T_.transpose(ps((j % 2) * 4 + k, i * P, P), RAW[j % 4][:, i, k * P:(k + 1) * P], ident[:, :])
                ins.then_inc(s["w_tr"], 1)
            pe.wait_ge(s["down_in"], 64)
            pe.wait_ge(s["w_lo"], 32)
            for m in range(16):
                q, t = m // 4, m % 4
                if m >= 8:
                    pe.wait_ge(s["dn_st"], m - 7)
                for i in range(4):
                    ins = T_.transpose(ps(m % 8, i * P, P), RAWD[t][:, (4 * q + i) * P:(4 * q + i + 1) * P], ident[:, :])
                ins.then_inc(s["dn_tr"], 1)
            pe.wait_ge(s["wd_lo"], 4)
            pe.wait_ge(s["pro_lo"], 2)
            pe.wait_ge(s["sel_done"], 1)

            def batch(it, ahead, fill):
                wait = per(pe, it, ahead)
                bank3 = [("xt_lo", 12, 12, -1) if fill else None]
                scored = [None]

                def take(last, *reader):
                    if last[0]:
                        wait(*last[0])
                    last[0] = reader

                def norm(u, t):
                    k = 4 * u + t
                    wait("xn_done", 12, k + 1)
                    take(bank3, "xt_lo", 12, k + 1)
                    for kc in range(KC):
                        ins = T_.transpose(ps(3, kc * P, P), xn[:, kc * P:(kc + 1) * P], ident[:, :])
                    ins.then_inc(s["xt_ps"], 1)

                def half_product(f, i, W, at):
                    th, c = i // HC, i % HC
                    for kc in range(KC):
                        ins = three(ps(4 + i % 2, at, TH), lambda q: W[:, q, kc, c * P:(c + 1) * P],
                                    lambda q: XT[f][:, q, kc, th * TH:(th + 1) * TH], kc == 0, kc == KC - 1)
                    return ins

                def gate(f, i):
                    if i >= 2:
                        wait(f"gated{f}", 32, i - 1, -f)
                    if i % HC == 0:
                        wait("xt_lo", 12, 8 * f + 2 * (i // HC + 1), -f)
                    half_product(f, i, WG, 0)

                def up(f, i):
                    half_product(f, i, WU, TH).then_inc(s[f"gu_ps{f}"], 1)

                def down(f, i):
                    th, c = i // HC, i % HC
                    wait(f"h_lo{f}", 32, i + 1, -f)
                    if c == 0 and th:
                        wait(("x1_done", "out_ready")[f], TT, 2, -f)
                    elif c == 0 and f == 0 and fill:
                        wait("x2_done", TT, TT, -1)
                    for t in range(2):
                        ins = three(ps(6 * f + t), lambda q: HP[i % 2][q][:, t * P:(t + 1) * P], lambda q: WD[:, q, c, :], c == 0, c == HC - 1)
                    ins.then_inc(s[f"down_done{f}"], 1)

                def qkv(hf, t):
                    i = hf * TT + t
                    if hf == 0:
                        wait("xt_lo", 12, 4 + t + 1)
                    if t:
                        wait("sq_done", 8, i)
                        wait("vlo_done", 8, i)
                    elif hf:
                        wait("phi_done", 16, HH)
                    else:
                        wait("x1_done", TT, TT)
                    for kc in range(KC):
                        ins = three(ps(0).rearrange("p (a n) -> p a n", a=2), lambda q: XT[0][:, q, kc, t * P:(t + 1) * P],
                                    lambda q: WQ[:, q, kc, 0:2 * D].rearrange("p (a n) -> p a n", a=2)[:, :, hf * 256:(hf + 1) * 256], kc == 0, kc == KC - 1)
                    ins.then_inc(s["qk_ps"], 1)
                    for kc in range(KC):
                        ins = three(ps(1, 0, 256), lambda q: XT[0][:, q, kc, t * P:(t + 1) * P],
                                    lambda q: WQ[:, q, kc, 2 * D + hf * 256:2 * D + (hf + 1) * 256], kc == 0, kc == KC - 1)
                    ins.then_inc(s["v_ps"], 1)

                def stack(hf, t):
                    i = hf * TT + t
                    wait("st_lo", 8, i + 1)
                    if t:
                        wait("qt_ev", 8, i)
                    for h in range(HH):
                        ins = T_.transpose(ps16(2)[0:ST, h * P:(h + 1) * P], STK[:, h, :], ident16[:, :])
                    ins.then_inc(s["qt_ps"], 1)
                    take(bank3, "kt_ev", 8, i + 1)
                    for h in range(HH):
                        ins = T_.transpose(ps16(3)[0:ST, h * P:(h + 1) * P], STK[:, HH + h, :], ident16[:, :])
                    ins.then_inc(s["kt_ps"], 1)

                def scores_max(hf, h):
                    k = hf * HH + h
                    if h == 0:
                        wait("qt_ev", 8, (hf + 1) * TT)
                        wait("kt_ev", 8, (hf + 1) * TT)
                        scored[0] = None
                    take(scored, "smax_done", 16, k + 1)
                    for t in (3, 2, 0, 1):
                        w = (t + 1) * P
                        T_.matmul(ps(0, QSEG[t], w), QT[0:ST, h, t * P:(t + 1) * P], KT[0:ST, h, 0:w], start=True, stop=False)
                        ins = T_.matmul(ps(0, QSEG[t] + t * P, P), identb[:, :], maskq[:, :], start=False, stop=True)
                    ins.then_inc(s["s1_ps"], 1)

                def max_rows(hf, g):
                    wait("mst_done", 4, hf * 2 + g + 1)
                    take(bank3, "mt_copied", 4, hf * 2 + g + 1)
                    for t in range(TT):
                        ins = T_.transpose(ps16(3)[ST:ST + MR, t * P:(t + 1) * P], mst[:, t * MR:(t + 1) * MR], ident16[:, :])
                    ins.then_inc(s["mt_ps"], 1)

                def scores(hf, h):
                    k = hf * HH + h
                    if h % GH == 0:
                        wait("mrow_done", 4, k // GH + 1)
                    take(scored, "phi_done", 16, k + 1)
                    for t in (0, 1, 3, 2):
                        w = (TT - t) * P
                        T_.matmul(ps(0, KSEG[t], w), KT[0:ST + MR, h, t * P:(t + 1) * P], QT[0:ST + MR, h, t * P:S], start=True, stop=False)
                        ins = T_.matmul(ps(0, KSEG[t], P), identb[:, :], maskk[:, :], start=False, stop=True)
                    ins.then_inc(s["s2_ps"], 1)

                def values(hf, h):
                    k = hf * HH + h
                    wait("plo_done", 16, k + 1)
                    take(bank3, "y_copied", 16, k + 1)
                    for t in range(TT):
                        for kt in range(t + 1):
                            c = KSEG[kt] + (t - kt) * P
                            T_.matmul(ps(3, t * YW, YW), PHI[:, c:c + P], V[:, kt, h, 0:YW], start=kt == 0, stop=False)
                            ins = T_.matmul(ps(3, t * YW + HD, HD + 1), PLO[:, c:c + P], V[:, kt, h, HD:YW], start=False, stop=kt == t)
                    ins.then_inc(s["pv_ps"], 1)

                def y_turn(hf, g):
                    k = hf * 2 + g
                    wait("ynorm_done", 16, GH * (k + 1))
                    take(bank3, "yt_lo", 4, k + 1)
                    for t in range(TT):
                        ins = T_.transpose(ps(3, t * P, P), Yf[:, t].rearrange("p h c -> p (h c)"), ident[:, :])
                    ins.then_inc(s["yt_ps"], 1)

                def out_product(_, t):
                    if t == 0:
                        wait("yt_lo", 4, 4)
                    if t == 3:
                        wait("x2_done", TT, 1)
                    for kc in range(KC):
                        ins = three(ps(t % 3), lambda q: YT[kc // 2][:, q, kc % 2, t * P:(t + 1) * P], lambda q: WO[:, q, kc, :], kc == 0, kc == KC - 1)
                    ins.then_inc(s["op_ps"], 1)

                run({"norm": norm, "gate": gate, "up": up, "down": down, "qkv": qkv, "stack": stack, "scores max": scores_max,
                     "max rows": max_rows, "scores": scores, "values": values, "y turn": y_turn, "out": out_product}, fill)

            batch(0, 0, False)
            with pe.Fori(0, B - 1) as it:
                batch(it, 1, True)
            batch(0, B, None)


_INS = ["L0_attn_x", "L0_attn_w_qkv", "L0_attn_w_out", "L0_attn_q_gain", "L0_ffn_w_gate", "L0_ffn_w_up", "L0_ffn_w_down"]


def rope_table():
    import numpy as np
    half = HD // 2
    freq = np.float32(10000.0) ** (-np.arange(half, dtype=np.float32) / np.float32(half))
    theta = np.arange(S, dtype=np.float32)[:, None] * freq[None, :]
    c, sn = np.cos(theta), np.sin(theta)
    return np.concatenate([c, c, -sn, sn], axis=1).astype(np.float32)


def kernel(**inputs):
    import numpy as np
    import concourse.bacc as bacc
    from concourse.bass_utils import run_bass_kernel_spmd

    nc = bacc.Bacc("TRN2", target_bir_lowering=False, num_devices=1)
    arrays, args = {}, []
    for name in _INS:
        a = np.ascontiguousarray(inputs[name])
        arrays[f"in_{name}"] = a
        args.append(nc.dram_tensor(f"in_{name}", a.shape, F32, kind="ExternalInput").ap())
    arrays["rope_table"] = rope_table()
    args.append(nc.dram_tensor("rope_table", (S, 64), F32, kind="ExternalInput").ap())
    args.append(nc.dram_tensor("out", (B, S, D), F32, kind="ExternalOutput").ap())
    build(nc, *args)
    r = run_bass_kernel_spmd(nc, [arrays], core_ids=[0])
    return r.results[0]["out"]
```

```python
import concourse.bass as bass
from concourse import mybir
from concourse.alu_op_type import AluOpType as ALU

ACT = mybir.ActivationFunctionType
AX_X = mybir.AxisListType.X
RMAX = bass.bass_isa.ReduceOp.max
F32, F16, BF16, I32 = mybir.dt.float32, mybir.dt.float16, mybir.dt.bfloat16, mybir.dt.int32

P = 128
B, S, D, H = 8, 512, 512, 16
HD = D // H
HID = 2048
KC = D // P
TT = S // P
HC = HID // P
HH = H // 2
TH = S // 2
QKV_UNITS = ((1, 2, 2, 3, 2), (1, 2, 2, 3, 3))
GH = 4
ST = 3 * HD
MR = 2 * GH
VW = 2 * HD + 2
YW = 2 * HD + 1
SW = P * TT * (TT + 1) // 2
LN_EPS, QK_EPS = 1e-5, 1e-6
LEAST = 2.0 ** -60
MASKED = -1e36
EXP_BITS = 0x7F800000
LN2 = 0.6931471805599453


def build(nc, x, w_qkv, w_out, q_gain, w_gate, w_up, w_down, rope, out):
    def sb(name, cols, dt):
        return nc.alloc_sbuf_tensor(name, [P, cols], dt)

    WG = sb("WG", 2 * KC * HID, F16)[:, :].rearrange("p (s k n) -> p s k n", s=2, k=KC)
    WU = sb("WU", 2 * KC * HID, F16)[:, :].rearrange("p (s k n) -> p s k n", s=2, k=KC)
    WD = sb("WD", 2 * HC * D, F16)[:, :].rearrange("p (s k n) -> p s k n", s=2, k=HC)
    WQ = sb("WQ", 2 * KC * 3 * D, F16)[:, :].rearrange("p (s k n) -> p s k n", s=2, k=KC)
    WO = sb("WO", 2 * KC * D, F16)[:, :].rearrange("p (s k n) -> p s k n", s=2, k=KC)

    at, place = 0, {}
    for name, words in (("xa", TT * D), ("xt", KC * S), ("ffn", 2 * TH + 2 * TH), ("xn", D), ("qt", HH * S // 2),
                        ("kt", HH * S // 2), ("xb", TT * D), ("v", TT * HH * VW // 2), ("work", 3332),
                        ("yt", S * 2), ("xt2", KC * S)):
        place[name] = (at, words)
        at += words
    arena = sb("arena", at, F32)

    def words(name, first=0, n=None):
        a, size = place[name]
        n = size - first if n is None else n
        assert first + n <= size
        return arena[:, a + first:a + first + n]

    def halves(name, first=0, n=None):
        return words(name, first, n).bitcast(F16)

    xa = words("xa").rearrange("p (t d) -> p t d", t=TT)
    xb = words("xb").rearrange("p (t d) -> p t d", t=TT)
    xn = [words("xn"), words("qt", 0, D)]
    XT = [halves(n).rearrange("p (s k n) -> p s k n", s=2, k=KC) for n in ("xt", "xt2")]
    YT = [halves(n, 0, 2 * S).rearrange("p (s k n) -> p s k n", s=2, k=2) for n in ("yt", "xt")]
    QT = halves("qt").rearrange("p (h n) -> p h n", h=HH)
    KT = halves("kt").rearrange("p (h n) -> p h n", h=HH)
    V = halves("v").rearrange("p (t h c) -> p t h c", t=TT, h=HH)
    P32 = words("work", 0, SW)
    PHI = halves("work", SW, SW // 2)
    PLO = halves("work", SW + SW // 2, SW // 2)
    Yf = [w.rearrange("p (t h c) -> p t h c", t=TT, h=GH) for w in (words("work", 2 * SW, TT * P), xn[0])]
    qs = [words("work", D * i, D) for i in range(2)]
    qn = [words("work", 2 * D + D * i, D) for i in range(2)]
    ropeU = words("work", 4 * D, D // 2)
    ropeV = words("work", 4 * D + D // 2, D // 2)
    STK = halves("work", 5 * D, HH * ST).rearrange("p (h c) -> p h c", h=2 * HH)
    fH = [words("ffn", TH * i, TH) for i in range(2)]
    HP = [[halves("ffn", 2 * TH + TH * q + TH // 2 * i, TH // 2) for q in range(2)] for i in range(2)]
    RAW = [arena[:, 2048 * (i + 1):2048 * (i + 2)].rearrange("p (i d) -> p i d", i=4) for i in range(4)]
    WD32 = arena[:, 2048:2048 + HC * D]
    assert place["v"][0] >= 2048 + HC * D and at - KC * 3 * D >= place["work"][0]
    RAWQ = arena[:, at - KC * 3 * D:at].rearrange("p (k n) -> p k n", k=KC)
    WDflat, WQflat = WD.rearrange("p s k n -> p (s k n)").bitcast(F32), WQ.rearrange("p s k n -> p (s k n)").bitcast(F32)
    RAWD = [WDflat[:, HID * i:HID * (i + 1)] for i in range(4)]
    RAWO = WQflat[:, 0:KC * D]

    ident = sb("ident", P, F32)
    ident16 = sb("ident16", P, F16)
    identb = sb("identb", P, BF16)
    maskq = sb("maskq", P, BF16)
    maskk = sb("maskk", P, BF16)
    ropet = sb("ropet", TT * 64, F32)
    ropev = ropet[:, :].rearrange("p (t c) -> p t c", t=TT)
    gain = sb("gain", 5 * H, F32)
    hscale = sb("hscale", H, F32)
    wmax = sb("wmax", 32, F32)
    wpow = sb("wpow", 32, F32)
    wrec = sb("wrec", 32, F32)
    wscale = sb("wscale", 32, F32)
    tscale = sb("tscale", HC, F32)
    pgu = sb("pgu", HC, F32)
    qmax = sb("qmax", KC, F32)
    gmax = sb("gmax", 3, F32)
    gall = sb("gall", 3, F32)
    gpow = sb("gpow", 3, F32)
    grec = sb("grec", 3, F32)
    gscale = sb("gscale", 3, F32)
    unscale = sb("unscale", 4, F32)
    stat = sb("stat", 6 * TT, F32)
    mv = sb("mv", 2 * TT, F32)
    var2 = sb("var2", TT, F32)
    rstd = sb("rstd", TT, F32)
    mhalf = sb("mhalf", 2 * HH, F32)
    ss = sb("ss", 4 * HH, F32)
    ss2 = sb("ss2", 4 * HH, F32)
    rn = sb("rn", 4 * HH, F32)
    mneg = sb("mneg", TT * HH, F32)
    mst = sb("mst", TT * MR, F16)
    yrec = sb("yrec", GH * TT, F32)
    carrier = sb("carrier", 3 * TT, F32)
    lnbias = sb("lnbias", 1, F32)

    psum = nc.alloc_psum_tensor("psum", [P, 8 * 512], F32)

    def ps(b, a=0, n=512):
        return psum[:, b * 512 + a:b * 512 + a + n]

    def ps16(b):
        return psum[:, b * 512:(b + 1) * 512].bitcast(F16)

    def turn_bank(u, t):
        return 2 if t % 2 and u != 2 else 3

    QSEG = {3: 0, 2: 512, 0: 896, 1: 1024}
    KSEG = {0: 0, 1: 512, 3: 896, 2: 1024}
    QBANKS, KBANKS = ((3,), (2, 0), (1,)), ((0,), (1, 3), (2,))
    PCOLS = (slice(0, 512), slice(512, SW))

    names = """c_in raw0 raw1 raw2 raw3 down_in qkv_in out_in c_made wscaled wsent w_tr w_hi w_lo
        dn_tr dn_st gmax_in gmax_all scales wd_hi wd_lo sel_done pro_hi pro_lo dve_pro pool_pro
        x_in0 x_in1 stored0 stored1 x1_done x2_done out_ready var_ready rstd_ready xn_done xt_ps xt_hi xt_lo
        qk_ps v_ps qs_done sq_done vhi_done vlo_done ssq_ready r_ready qn_done rope_done
        st_hi st_lo qt_ps kt_ps qt_ev kt_ev s1_ps smax_done mst_done mt_ps mt_copied mrow_done
        s2_ps phi_done plo_done pv_ps y_read ynorm_done yt_ps yt_hi yt_lo op_ps
        gu_ps tanh_done a_done gated h_hi h_lo down_done dve_chain pool_chain"""
    s = {n: nc.alloc_semaphore(n) for n in names.split()}

    def per(eng, it, ahead):
        def wait(name, n, k, batch=0):
            eng.wait_ge(s[name], it * n + (ahead + batch) * n + k)
        return wait

    def per_step(wait, fill):
        place_of = {fi: j for j, fi in enumerate(stream(fill))}

        def step(name, f, i, back=0):
            j = place_of[f, i] - back
            if fill is not False:
                wait(name, 2 * STEPS, j + 1 - STEPS)
            elif j >= 0:
                wait(name, 2 * STEPS, j + 1)
        return step

    STEPS = 2 * HC
    AHEAD = 2

    def stream(fill):
        first = [(0, i) for i in range(STEPS)] if fill is not None else []
        second = [(1, i) for i in range(STEPS)] if fill is not False else []
        return second[:AHEAD] + first + second[AHEAD:]

    def ffn_units(steps, j):
        n = len(steps)
        down = [("down",) + steps[j - 2]] if j >= 2 else []
        gate, up = ([[(name,) + steps[j]] for name in ("gate", "up")] if j < n else ([], []))
        units = [gate, up, down] if down and down[0][2] == HC else [down, gate, up]
        if 1 <= j <= n:
            units[0] = units[0] + [("gated",) + steps[j - 1]]
            units[1] = units[1] + [("parts",) + steps[j - 1]]
        if down and down[0][2] % HC == HC - 1:
            units[2] = units[2] + [("residual", down[0][1], down[0][2] // HC)]
        if j >= n:
            units = [sum(units, [])]
        return [u for u in units if u]

    def order(fill):
        o = []
        steps = stream(fill)
        units = [ffn_units(steps, j) for j in range(len(steps) + 2)]
        if fill is None:
            before = {0: [("norm", 3, 2), ("turn", 3, 2), ("norm", 3, 3), ("split", 3, 2)], 1: [("turn", 3, 3), ("split", 3, 3)]}
            for j, point in enumerate(units):
                o += sum(point, []) + before.get(j, [])
            return o

        def point():
            o.extend(sum(units.pop(0), []))

        if fill:
            (g0, u0), (a0, g1, u1), (d0, g2, u2) = (units.pop(0) for _ in range(3))
            o += [("norm", 3, 2), ("stats", 0, 0)] + g0 + [("turn", 3, 2), ("norm", 3, 3), ("stats", 0, 1), ("split", 3, 2)]
            o += u0 + [("turn", 3, 3), ("norm", 0, 0), ("split", 3, 3)] + a0 + g1
            o += [("turn", 0, 0), ("norm", 0, 1), ("split", 0, 0)] + u1
            o += [("turn", 0, 1)] + d0 + [("split", 0, 1)] + g2 + u2
        else:
            o += [("stats", 0, 0), ("stats", 0, 1), ("norm", 0, 0), ("turn", 0, 0), ("norm", 0, 1), ("split", 0, 0),
                  ("turn", 0, 1), ("split", 0, 1)]
            point()
        late = {0: [("stats", 0, 2)], 1: [("norm", 0, 2), ("turn", 0, 2), ("stats", 0, 3)],
                2: [("split", 0, 2), ("norm", 0, 3), ("turn", 0, 3)], 3: [("split", 0, 3)],
                HC + 2: [("stats", 1, 0)], HC + 3: [("norm", 1, 0), ("turn", 1, 0), ("stats", 1, 1)], HC + 4: [("split", 1, 0)],
                HC + 5: [("norm", 1, 1), ("turn", 1, 1)], HC + 6: [("split", 1, 1)]}
        if not fill:
            late.update({4: [("magnitude", 0, 0)], 5: [("magnitude", 0, 1)], 6: [("magnitude", 0, 2)],
                         7: [("magnitude", 0, 3)], 8: [("magnitude", 1, 0)], 10: [("scales", 0, 0)], 11: [("pickers", 0, 0)], 12: [("weights", 1, 0)],
                         14: [("weights", 0, 0)], 15: [("weights", 0, 1)], 16: [("weights", 0, 2)], 17: [("weights", 0, 3)]})
        for i in range(STEPS + 2):
            if i:
                point()
            o += late.get(i, [])
        pieces = sum(units, [])

        def some(n=1):
            for _ in range(n):
                if len(pieces) > 1:
                    o.extend(pieces.pop(0))

        some(2)
        o += [("stats", 1, 2), ("stats", 1, 3)]
        some(1)
        for hf in range(2):
            turns = []
            for t in range(TT + 1):
                if t < TT:
                    o.append(("qkv", hf, t))
                o += turns
                turns = []
                if t:
                    o.append(("unit", hf, t - 1))
                if hf == 0 and t == 0:
                    o += [("norm", 1, 2), ("turn", 1, 2), ("norm", 1, 3), ("split", 1, 2)]
                if t < TT:
                    o.append(("qkv out", hf, t))
                else:
                    some(2)
                if t == 0:
                    o += [("y turn", 0, 1)] if hf else []
                    some()
                    o += [] if hf else [("turn", 1, 3), ("split", 1, 3)]
                if t:
                    o.append(("stack", hf, t - 1))
                some(QKV_UNITS[hf][t])
                if t:
                    turns = [("stack turn", hf, t - 1), ("stack out", hf, t - 1)]
                if fill or t == TT:
                    o += turns
                    turns = []
            some()
            for h in range(GH):
                o += [("scores max", hf, h), ("row max", hf, h)]
                if h == GH - 1:
                    o.append(("maxima", hf, 0))
                some()
            o.append(("max rows", hf, 0))
            some()
            for h in range(HH):
                o.append(("scores", hf, h))
                if h:
                    o += [("values", hf, h - 1), ("y out", hf, h - 1)]
                o.append(("exp", hf, h))
                some()
                if h == GH + 1:
                    o.append(("y turn", hf, 0))
                if h < GH:
                    some()
                    o += [("scores max", hf, GH + h), ("row max", hf, GH + h)]
                    if h == GH - 1:
                        o.append(("maxima", hf, 1))
                    some()
                else:
                    some()
                if h == GH - 1:
                    o.append(("max rows", hf, 1))
                    some()
            if hf == 0:
                some()
            else:
                o.append(("out part", 0, 0))
            o += [("values", hf, HH - 1), ("y out", hf, HH - 1)]
        o += sum(pieces, [])
        o += [("out part", 0, 1), ("y turn", 1, 1), ("out part", 0, 2), ("out", 0, 0), ("out residual", 0, 0), ("stats", 2, 0),
              ("out", 0, 1), ("out residual", 0, 1), ("norm", 2, 0), ("out", 0, 2), ("stats", 2, 1),
              ("out part", 0, 3), ("turn", 2, 0), ("norm", 2, 1), ("out residual", 0, 2), ("split", 2, 0),
              ("out", 0, 3), ("turn", 2, 1), ("out residual", 0, 3), ("split", 2, 1), ("stats", 2, 2), ("stats", 2, 3)]
        return o

    def run(stages, fill):
        for name, a, b in order(fill):
            if name in stages:
                stages[name](a, b)

    with nc.Block() as block:

        @block.sync
        def _(sp):
            def half_of(batch, th):
                return batch[th * TH:(th + 1) * TH, :].rearrange("(t p) d -> p t d", p=P)

            sp.dma_start(ropev, rope.rearrange("(t p) c -> p t c", p=P)).then_inc(s["c_in"], 16)
            sp.dma_start(gain[:, 0:H], q_gain.rearrange("(a n) -> a n", a=1).broadcast_to([P, H])).then_inc(s["c_in"], 16)
            for j in range(8):
                w = (w_gate if j < 4 else w_up)[(j % 4) * 512:(j % 4 + 1) * 512, :]
                if j >= 4:
                    sp.wait_ge(s["w_tr"], j - 3)
                sp.dma_start(RAW[j % 4], w.rearrange("(i p) d -> p i d", p=P)).then_inc(s[f"raw{j % 4}"], 16)
                if j >= 4:
                    t = j - 4
                    sp.dma_start(RAWD[t], w_down[t * P:(t + 1) * P, :]).then_inc(s["down_in"], 16)
            sp.dma_start(RAWQ, w_qkv.rearrange("(k p) n -> p k n", p=P)).then_inc(s["qkv_in"], 16)
            sp.dma_start(RAWO.rearrange("p (k n) -> p k n", k=KC), w_out.rearrange("(k p) n -> p k n", p=P)).then_inc(s["out_in"], 16)
            for th in range(2):
                sp.dma_start(xa[:, 2 * th:2 * th + 2, :], half_of(x[0], th)).then_inc(s[f"x_in{th}"], 16)
            with sp.Fori(0, B - 1) as it:
                for th in range(2):
                    sp.wait_ge(s["x2_done"], it * TT + 2 * th + 2)
                    sp.dma_start(xa[:, 2 * th:2 * th + 2, :], half_of(x[it + 1], th)).then_inc(s[f"x_in{th}"], 16)
                for th in range(2):
                    sp.wait_ge(s["out_ready"], it * TT + 2 * th + 2)
                    sp.dma_start(half_of(out[it], th), xb[:, 2 * th:2 * th + 2, :]).then_inc(s[f"stored{th}"], 16)
            for th in range(2):
                sp.wait_ge(s["out_ready"], (B - 1) * TT + 2 * th + 2)
                sp.dma_start(half_of(out[B - 1], th), xb[:, 2 * th:2 * th + 2, :]).then_inc(s[f"stored{th}"], 16)
            for th in range(2):
                sp.wait_ge(s[f"stored{th}"], 16 * B)

        @block.gpsimd
        def _(pool):
            n = [0]

            def link(ins):
                n[0] += 1
                ins.then_inc(s["pool_pro"], 1)
                pool.wait_ge(s["pool_pro"], n[0])

            for m in (ident, ident16, identb, maskq, maskk):
                link(nc.gpsimd.memset(m[:, :], 0.0))
            link(nc.gpsimd.memset(mhalf[:, :], -0.5))
            link(nc.gpsimd.memset(mst[:, :], 0.0))
            link(nc.gpsimd.memset(halves("v"), 1.0))
            for m in (ident, ident16, identb):
                link(nc.gpsimd.affine_select(out=m[:, :], in_=m[:, :], compare_op=ALU.not_equal, fill=1.0,
                                             base=0, pattern=[[-1, P]], channel_multiplier=1))
            link(nc.gpsimd.affine_select(out=maskq[:, :], in_=maskq[:, :], compare_op=ALU.is_ge, fill=MASKED,
                                         base=0, pattern=[[-1, P]], channel_multiplier=1))
            nc.gpsimd.affine_select(out=maskk[:, :], in_=maskk[:, :], compare_op=ALU.is_ge, fill=MASKED,
                                    base=0, pattern=[[1, P]], channel_multiplier=-1).then_inc(s["c_made"], 1)
            pool.wait_ge(s["gmax_in"], 1)
            nc.gpsimd.partition_all_reduce(gall[:, 0:1], gmax[:, 0:1], P, RMAX).then_inc(s["gmax_all"], 1)
            def batch(it, ahead, fill):
                wait = per(pool, it, ahead)
                turns = [0]

                def stats(u, t):
                    wait("var_ready", 12, 4 * u + t + 1)
                    nc.gpsimd.tensor_tensor(rstd[:, t:t + 1], var2[:, t:t + 1], mhalf[:, 0:1], ALU.pow).then_inc(s["rstd_ready"], 1)

                def qkv_out(hf, t):
                    i, c = hf * TT + t, slice(16 * (t % 2), 16 * (t % 2) + 16)
                    wait("ssq_ready", 8, i + 1)
                    nc.gpsimd.tensor_tensor(rn[:, c], ss2[:, c], mhalf[:, :], ALU.pow).then_inc(s["r_ready"], 1)

                def rotate(hf, t):
                    i = hf * TT + t
                    wait("qn_done", 8, i + 1)
                    ev = qn[t % 2].rearrange("p (e o c) -> p e o c", o=2, c=HD)[:, :, 0, :]
                    U = ropeU.rearrange("p (e c) -> p e c", c=HD)
                    W = ropeV.rearrange("p (e c) -> p e c", c=HD)
                    hw = HD // 2

                    def table(a, w):
                        return ropev[:, t, a:a + w].unsqueeze(1).broadcast_to([P, HH, w])

                    nc.gpsimd.tensor_tensor(U, ev, table(0, HD), ALU.mult)
                    nc.gpsimd.tensor_tensor(W[:, :, 0:hw], ev[:, :, hw:HD], table(HD, hw), ALU.mult)
                    turns[0] += 1
                    nc.gpsimd.tensor_tensor(W[:, :, hw:HD], ev[:, :, 0:hw], table(HD + hw, hw), ALU.mult).then_inc(s["pool_chain"], 1)
                    wait("pool_chain", 8, turns[0])
                    nc.gpsimd.tensor_tensor(ev, U, W, ALU.add).then_inc(s["rope_done"], 1)

                def scales(*_):
                    pool.wait_ge(s["gmax_in"], 3)
                    nc.gpsimd.partition_all_reduce(gall[:, 1:3], gmax[:, 1:3], P, RMAX).then_inc(s["gmax_all"], 1)

                def pickers(*_):
                    pool.wait_ge(s["wd_lo"], 4)
                    pool.wait_ge(s["gmax_all"], 2)
                    kr = KT[ST:ST + MR, :, :]
                    krv = kr.rearrange("p (a g) n -> p a g n", g=GH)
                    link(nc.gpsimd.memset(kr, 4096.0))
                    link(nc.gpsimd.affine_select(out=krv, in_=krv, compare_op=ALU.is_ge, fill=0.0, base=0,
                                                 pattern=[[0, 2], [-2, GH], [0, S]], channel_multiplier=1))
                    nc.gpsimd.affine_select(out=krv, in_=krv, compare_op=ALU.is_ge, fill=0.0, base=1,
                                            pattern=[[0, 2], [2, GH], [0, S]], channel_multiplier=-1).then_inc(s["sel_done"], 1)
                    pool.wait_ge(s["sel_done"], 1)

                run({"stats": stats, "qkv out": qkv_out, "unit": rotate, "scales": scales, "pickers": pickers}, fill)

            batch(0, 0, False)
            with pool.Fori(0, B - 1) as it:
                batch(it, 1, True)

        @block.scalar
        def _(act):
            def scale_rows(j):
                act.wait_ge(s["wsent"], j + 1)
                for i in range(4):
                    c, r = 4 * j + i, RAW[j % 4][:, i, :]
                    ins = nc.scalar.activation(r, r, ACT.Copy, scale=wscale[:, c:c + 1])
                ins.then_inc(s["wscaled"], 1)

            scale_rows(0)
            for j in range(8):
                if j + 1 < 8:
                    scale_rows(j + 1)
                act.wait_ge(s["w_tr"], j + 1)
                W = WG if j < 4 else WU
                for k in range(KC):
                    nc.scalar.activation(W[:, 0, k, (j % 4) * 512:(j % 4 + 1) * 512], ps((j % 2) * 4 + k), ACT.Copy).then_inc(s["w_hi"], 1)
            act.wait_ge(s["scales"], 1)
            for q in range(4):
                nc.scalar.activation(WD[:, 0, 4 * q:4 * q + 4, :], WD32[:, 2048 * q:2048 * (q + 1)].rearrange("p (k n) -> p k n", n=D),
                                     ACT.Copy, scale=gscale[:, 0:1]).then_inc(s["wd_hi"], 1)

            def batch(it, ahead, fill):
                wait = per(act, it, ahead)
                step = per_step(wait, fill)

                def split(u, t):
                    if u < 3:
                        wait("xt_ps", 12, 4 * u + t + 1)
                    else:
                        wait("xt_ps", 12, 8 + t + 1, -1)
                    nc.scalar.activation(XT[u // 2][:, 0, :, t * P:(t + 1) * P], ps(turn_bank(u, t)).rearrange("p (k n) -> p k n", k=KC), ACT.Copy).then_inc(s["xt_hi"], 1)

                def qkv_out(hf, t):
                    i, b2 = hf * TT + t, t % 2
                    wait("qk_ps", 8, i + 1)
                    if t >= 2:
                        wait("st_lo", 8, i - 1)
                    nc.scalar.activation(qn[b2], ps(0), ACT.Square, scale=unscale[:, 1:2]).then_inc(s["sq_done"], 1)
                    nc.scalar.activation(qs[b2], ps(0), ACT.Copy, scale=unscale[:, 1:2]).then_inc(s["qs_done"], 1)
                    wait("v_ps", 8, i + 1)
                    nc.scalar.activation(V[:, t, :, HD:2 * HD], ps(1, 0, 256).rearrange("p (h c) -> p h c", c=HD),
                                         ACT.Copy, scale=2.0 ** -17).then_inc(s["vhi_done"], 1)

                def stack(hf, t):
                    i = hf * TT + t
                    wait("rope_done", 8, i + 1)
                    if t:
                        wait("kt_ps", 8, i)
                    q3 = qn[t % 2].rearrange("p (h c) -> p h c", c=HD)
                    nc.scalar.activation(STK[:, :, 0:HD], q3, ACT.Copy)
                    nc.scalar.activation(STK[:, 0:HH, HD:2 * HD], q3[:, 0:HH, :], ACT.Copy)
                    nc.scalar.activation(STK[:, HH:2 * HH, 2 * HD:ST], q3[:, HH:2 * HH, :], ACT.Copy).then_inc(s["st_hi"], 1)

                def stack_out(hf, t):
                    wait("qt_ps", 8, hf * TT + t + 1)
                    nc.scalar.activation(QT[0:ST, :, t * P:(t + 1) * P], ps16(2)[0:ST, :].rearrange("p (h n) -> p h n", h=HH),
                                         ACT.Copy).then_inc(s["qt_ev"], 1)

                def max_rows(hf, g):
                    wait("mt_ps", 4, hf * 2 + g + 1)
                    nc.scalar.activation(QT[ST:ST + MR, g * GH, :], ps16(3)[ST:ST + MR, 0:S], ACT.Copy).then_inc(s["mt_copied"], 1)

                def exp(hf, h):
                    k = hf * HH + h
                    for m, c in enumerate(PCOLS):
                        wait("s2_ps", 32, 2 * k + m + 1)
                        if k:
                            wait("plo_done", 32, 2 * k - 1 + m)
                        nc.scalar.activation(P32[:, c], ps(0, 0, SW)[:, c], ACT.Exp, bias=lnbias[:, 0:1], scale=hscale[:, k:k + 1])
                    if k:
                        wait("pv_ps", 16, k)
                    for c in PCOLS:
                        nc.scalar.activation(PHI[:, c], ps(0, 0, SW)[:, c], ACT.Exp, bias=lnbias[:, 0:1],
                                             scale=hscale[:, k:k + 1]).then_inc(s["phi_done"], 1)

                def y_turn(hf, g):
                    k = hf * 2 + g
                    wait("yt_ps", 4, k + 1)
                    nc.scalar.activation(YT[hf][:, 0, g, :], ps(3), ACT.Copy).then_inc(s["yt_hi"], 1)

                def gated(f, i):
                    step("gu_ps", f, i)
                    step("h_lo", f, i, 2)
                    nc.scalar.activation(fH[i % 2], ps(4 + i % 2, 0, TH), ACT.Tanh, scale=tscale[:, i % HC:i % HC + 1]).then_inc(s["tanh_done"], 1)

                def parts(f, i):
                    step("gated", f, i)
                    step("down_done", f, i, 2)
                    nc.scalar.activation(HP[i % 2][0], fH[i % 2], ACT.Copy).then_inc(s["h_hi"], 1)

                def weights(out_, k):
                    if out_:
                        act.wait_ge(s["scales"], 2)
                        nc.scalar.activation(WO[:, 0], RAWO.rearrange("p (k n) -> p k n", k=KC), ACT.Copy, scale=gscale[:, 2:3]).then_inc(s["pro_hi"], 1)
                    else:
                        act.wait_ge(s["pro_lo"], 1)
                        nc.scalar.activation(WQ[:, 0, k], RAWQ[:, k], ACT.Copy, scale=gscale[:, 1:2]).then_inc(s["pro_hi"], 1)

                run({"split": split, "qkv out": qkv_out, "stack": stack, "stack out": stack_out, "max rows": max_rows,
                     "weights": weights,
                     "exp": exp, "y turn": y_turn, "gated": gated, "parts": parts}, fill)

            batch(0, 0, False)
            with act.Fori(0, B - 1) as it:
                batch(it, 1, True)
            batch(0, B, None)

        @block.vector
        def _(dve):
            V_ = nc.vector
            n = [0]

            def link(ins):
                n[0] += 1
                ins.then_inc(s["dve_pro"], 1)
                dve.wait_ge(s["dve_pro"], n[0])

            def power_of_two(out, in_):
                link(V_.tensor_scalar(out, in_, LEAST, None, ALU.max))
                link(V_.tensor_scalar(out.bitcast(I32), out.bitcast(I32), EXP_BITS, None, ALU.bitwise_and))

            link(V_.memset(lnbias[:, :], 14 * LN2))
            dve.wait_ge(s["c_in"], 32)
            g0, g1, g2, g3, g4 = (gain[:, i * H:(i + 1) * H] for i in range(5))
            link(V_.tensor_scalar(g1.bitcast(I32), g0.bitcast(I32), 0x7FFFFFFF, None, ALU.bitwise_and))
            power_of_two(g2, g1)
            link(V_.reciprocal(g3, g2))
            link(V_.tensor_tensor(g4, g0, g3, ALU.mult))
            link(V_.tensor_scalar(hscale[:, :], g2, 2.0 ** -24, None, ALU.mult))

            def w_scales(j):
                c = slice(4 * j, 4 * j + 4)
                dve.wait_ge(s[f"raw{j % 4}"], 16 * (j // 4 + 1))
                link(V_.tensor_reduce(wmax[:, c], RAW[j % 4], AX_X, ALU.max, apply_absolute_value=True))
                power_of_two(wpow[:, c], wmax[:, c])
                link(V_.reciprocal(wrec[:, c], wpow[:, c]))
                V_.tensor_scalar(wscale[:, c], wrec[:, c], 2.0 ** 13, None, ALU.mult).then_inc(s["wsent"], 1)

            w_scales(0)
            w_scales(1)
            for j in range(8):
                if j + 2 < 8:
                    w_scales(j + 2)
                W = WG if j < 4 else WU
                for k in range(KC):
                    dve.wait_ge(s["w_hi"], 4 * j + k + 1)
                    c = slice((j % 4) * 512, (j % 4 + 1) * 512)
                    V_.tensor_tensor(W[:, 1, k, c], ps((j % 2) * 4 + k), W[:, 0, k, c], ALU.subtract).then_inc(s["w_lo"], 1)
            link(V_.tensor_scalar(tscale[:, :], wpow[:, 0:HC], 2.0 ** -23, None, ALU.mult))
            link(V_.scalar_tensor_tensor(out=pgu[:, :], in0=wpow[:, 0:HC], scalar=2.0 ** 5, in1=wpow[:, HC:2 * HC], op0=ALU.mult, op1=ALU.mult))
            WD32v = WD32.rearrange("p (k n) -> p k n", n=D)
            for m in range(16):
                q, t = m // 4, m % 4
                dve.wait_ge(s["dn_tr"], m + 1)
                ins = V_.tensor_tensor(WD32v[:, 4 * q:4 * q + 4, t * P:(t + 1) * P], ps(m % 8).rearrange("p (k n) -> p k n", n=P),
                                       pgu[:, 4 * q:4 * q + 4].unsqueeze(2).broadcast_to([P, 4, P]), ALU.mult)
                ins.then_inc(s["dn_st"], 1)
            dve.wait_ge(s["dn_st"], 16)
            V_.tensor_reduce(gmax[:, 0:1], WD32, AX_X, ALU.max, apply_absolute_value=True).then_inc(s["gmax_in"], 1)
            dve.wait_ge(s["gmax_all"], 1)
            power_of_two(gpow[:, 0:1], gall[:, 0:1])
            link(V_.reciprocal(grec[:, 0:1], gpow[:, 0:1]))
            link(V_.tensor_scalar(unscale[:, 0:1], gpow[:, 0:1], 2.0 ** -14, None, ALU.mult))
            V_.tensor_scalar(gscale[:, 0:1], grec[:, 0:1], 2.0 ** 13, None, ALU.mult).then_inc(s["scales"], 1)
            dve.wait_ge(s["scales"], 1)
            for q in range(4):
                dve.wait_ge(s["wd_hi"], q + 1)
                V_.scalar_tensor_tensor(out=WD[:, 1, 4 * q:4 * q + 4, :].rearrange("p k n -> p (k n)"), in0=WD32[:, 2048 * q:2048 * (q + 1)], scalar=gscale[:, 0:1],
                                        in1=WD[:, 0, 4 * q:4 * q + 4, :].rearrange("p k n -> p (k n)"), op0=ALU.mult, op1=ALU.subtract).then_inc(s["wd_lo"], 1)
            pro_link = link

            LINKS = 3 * TT * 2 + 2 * TT * 2 + 4 + H * 2

            def batch(it, ahead, fill):
                wait = per(dve, it, ahead)
                step = per_step(wait, fill)
                n = [0]

                def link(ins):
                    n[0] += 1
                    ins.then_inc(s["dve_chain"], 1)
                    wait("dve_chain", LINKS, n[0])

                def stats(u, t):
                    src = (xa, xa, xb)[u]
                    if u == 0:
                        wait(f"x_in{t // 2}", 16, 16)
                    else:
                        wait(f"x{u}_done", TT, t + 1)
                    n[0] += 1
                    V_.bn_stats(stat[:, 6 * t:6 * t + 6], src[:, t, :]).then_inc(s["dve_chain"], 1)
                    wait("dve_chain", LINKS, n[0])
                    V_.memset(carrier[:, 4 * u + t:4 * u + t + 1], 0.0)
                    link(V_.bn_aggr(mv[:, 2 * t:2 * t + 2], stat[:, 6 * t:6 * t + 6]))
                    V_.tensor_scalar(var2[:, t:t + 1], mv[:, 2 * t + 1:2 * t + 2], LN_EPS, 2.0 ** -18, ALU.add, ALU.mult).then_inc(s["var_ready"], 1)

                def norm(u, t):
                    src = (xa, xa, xb, xb)[u]
                    k, batch = (4 * u + t, 0) if u < 3 else (8 + t, -1)
                    wait("rstd_ready", 12, k + 1, batch)
                    if k >= 2 or fill is not False:
                        wait("xt_ps", 12, k - 1, batch)
                    if t % 2 and u == 2:
                        wait("s2_ps", 32, 32)
                    V_.tensor_scalar(xn[t % 2], src[:, t, :], mv[:, 2 * t:2 * t + 1], rstd[:, t:t + 1], ALU.subtract, ALU.mult).then_inc(s["xn_done"], 1)

                def split(u, t):
                    if u < 3:
                        wait("xt_hi", 12, 4 * u + t + 1)
                    else:
                        wait("xt_hi", 12, 8 + t + 1, -1)
                    c = slice(t * P, (t + 1) * P)
                    V_.tensor_tensor(XT[u // 2][:, 1, :, c], ps(turn_bank(u, t)).rearrange("p (k n) -> p k n", k=KC), XT[u // 2][:, 0, :, c], ALU.subtract).then_inc(s["xt_lo"], 1)

                def gated(f, i):
                    g, u = ps(4 + i % 2, 0, TH), ps(4 + i % 2, TH, TH)
                    step("tanh_done", f, i)
                    V_.scalar_tensor_tensor(out=fH[i % 2], in0=fH[i % 2], scalar=1.0, in1=g, op0=ALU.add, op1=ALU.mult).then_inc(s["a_done"], 1)
                    step("a_done", f, i)
                    V_.scalar_tensor_tensor(out=fH[i % 2], in0=fH[i % 2], scalar=2.0 ** -50, in1=u, op0=ALU.mult, op1=ALU.mult).then_inc(s["gated"], 1)

                def parts(f, i):
                    step("h_hi", f, i)
                    V_.tensor_tensor(HP[i % 2][1], fH[i % 2], HP[i % 2][0], ALU.subtract).then_inc(s["h_lo"], 1)

                def residual(f, th):
                    step("down_done", f, HC * (th + 1) - 1)
                    dst, name = ((xa, "x1_done"), (xb, "out_ready"))[f]
                    for t in (2 * th, 2 * th + 1):
                        V_.scalar_tensor_tensor(out=dst[:, t, :], in0=ps(6 * f + t % 2), scalar=unscale[:, 0:1], in1=dst[:, t, :],
                                                op0=ALU.mult, op1=ALU.add).then_inc(s[name], 1)

                def qkv_out(hf, t):
                    i, c = hf * TT + t, slice(16 * (t % 2), 16 * (t % 2) + 16)
                    wait("sq_done", 8, i + 1)
                    link(V_.tensor_reduce(ss[:, c], qn[t % 2].rearrange("p (h c) -> p h c", c=HD), AX_X, ALU.add))
                    V_.tensor_scalar(ss2[:, c], ss[:, c], QK_EPS, 2.0 ** -24, ALU.add, ALU.mult).then_inc(s["ssq_ready"], 1)
                    wait("vhi_done", 8, i + 1)
                    V_.scalar_tensor_tensor(out=V[:, t, :, 0:HD], in0=ps(1, 0, 256).rearrange("p (h c) -> p h c", c=HD), scalar=2.0 ** -17,
                                            in1=V[:, t, :, HD:2 * HD], op0=ALU.mult, op1=ALU.subtract).then_inc(s["vlo_done"], 1)

                def unit(hf, t):
                    i, b2 = hf * TT + t, t % 2
                    wait("r_ready", 8, i + 1)
                    wait("qs_done", 8, i + 1)
                    link(V_.tensor_tensor(rn[:, 16 * b2:16 * b2 + HH], rn[:, 16 * b2:16 * b2 + HH], gain[:, 4 * H + hf * HH:4 * H + (hf + 1) * HH], ALU.mult))
                    V_.tensor_tensor(qn[b2].rearrange("p (h c) -> p h c", c=HD), qs[b2].rearrange("p (h c) -> p h c", c=HD),
                                     rn[:, 16 * b2:16 * b2 + 16].unsqueeze(2).broadcast_to([P, 2 * HH, HD]), ALU.mult).then_inc(s["qn_done"], 1)

                def stack(hf, t):
                    wait("st_hi", 8, hf * TT + t + 1)
                    q3 = qn[t % 2].rearrange("p (h c) -> p h c", c=HD)
                    V_.tensor_tensor(STK[:, 0:HH, 2 * HD:ST], q3[:, 0:HH, :], STK[:, 0:HH, 0:HD], ALU.subtract)
                    V_.tensor_tensor(STK[:, HH:2 * HH, HD:2 * HD], q3[:, HH:2 * HH, :], STK[:, HH:2 * HH, 0:HD], ALU.subtract).then_inc(s["st_lo"], 1)

                def stack_out(hf, t):
                    wait("kt_ps", 8, hf * TT + t + 1)
                    V_.tensor_copy(KT[0:ST, :, t * P:(t + 1) * P], ps16(3)[0:ST, :].rearrange("p (h n) -> p h n", h=HH)).then_inc(s["kt_ev"], 1)

                mnegv = mneg[:, :].rearrange("p (t h) -> p t h", t=TT)
                mstv = mst[:, :].rearrange("p (t h c) -> p t h c", t=TT, c=2)

                def row_max(hf, h):
                    for bank, tiles in enumerate(QBANKS):
                        wait("s1_ps", 48, 3 * (hf * HH + h) + bank + 1)
                        for t in tiles:
                            ins = V_.tensor_reduce(mnegv[:, t, h:h + 1], ps(0, QSEG[t], (t + 1) * P), AX_X, ALU.max, negate=True)
                        ins.then_inc(s["smax_done"], 1)

                def maxima(hf, g):
                    k = hf * 2 + g
                    wait("smax_done", 48, 3 * (hf * HH + (g + 1) * GH))
                    if k:
                        wait("mt_ps", 4, k)
                    src = mnegv[:, :, g * GH:(g + 1) * GH]
                    link(V_.tensor_scalar(mstv[:, :, :, 0], src, 2.0 ** -12, None, ALU.mult))
                    V_.scalar_tensor_tensor(out=mstv[:, :, :, 1], in0=src, scalar=2.0 ** -12, in1=mstv[:, :, :, 0], op0=ALU.mult, op1=ALU.subtract).then_inc(s["mst_done"], 1)

                def max_rows(hf, g):
                    wait("mt_copied", 4, hf * 2 + g + 1)
                    V_.tensor_copy(QT[ST:ST + MR, g * GH + 1:(g + 1) * GH, :],
                                   QT[ST:ST + MR, g * GH, :].unsqueeze(1).broadcast_to([MR, GH - 1, S])).then_inc(s["mrow_done"], 1)

                def exp(hf, h):
                    for m, c in enumerate(PCOLS):
                        wait("phi_done", 32, 2 * (hf * HH + h) + m + 1)
                        V_.tensor_tensor(PLO[:, c], P32[:, c], PHI[:, c], ALU.subtract).then_inc(s["plo_done"], 1)

                def y_out(hf, h):
                    wait("pv_ps", 16, hf * HH + h + 1)
                    if h % GH == 0 and hf:
                        wait("yt_ps", 4, h // GH + 1)
                    yv = Yf[h // GH][:, :, h % GH, :]
                    yp = ps(3, 0, TT * YW).rearrange("p (t c) -> p t c", t=TT)
                    n[0] += 1
                    rec = yrec[:, h % GH * TT:(h % GH + 1) * TT]
                    V_.reciprocal(rec, yp[:, :, 2 * HD]).then_inc(s["dve_chain"], 1)
                    link(V_.tensor_copy(yv, yp[:, :, 0:HD]))
                    V_.tensor_tensor(yv, yp[:, :, HD:2 * HD], yv, ALU.add).then_inc(s["y_read"], 1)
                    wait("y_read", 16, hf * HH + h + 1)
                    V_.tensor_tensor(yv, yv, rec.unsqueeze(2).broadcast_to([P, TT, HD]), ALU.mult).then_inc(s["ynorm_done"], 1)

                def y_turn(hf, g):
                    wait("yt_hi", 4, hf * 2 + g + 1)
                    V_.tensor_tensor(YT[hf][:, 1, g, :], ps(3), YT[hf][:, 0, g, :], ALU.subtract).then_inc(s["yt_lo"], 1)

                def out_residual(_, t):
                    wait("op_ps", TT, t + 1)
                    if t % 2 == 0 and fill:
                        wait(f"stored{t // 2}", 16, 16, -1)
                    V_.scalar_tensor_tensor(out=xb[:, t, :], in0=ps(t % 3), scalar=unscale[:, 2:3], in1=xa[:, t, :], op0=ALU.mult, op1=ALU.add).then_inc(s["x2_done"], 1)

                def magnitude(out_, k):
                    dve.wait_ge(s["out_in" if out_ else "qkv_in"], 16)
                    if out_:
                        pro_link(V_.tensor_reduce(gmax[:, 2:3], RAWO, AX_X, ALU.max, apply_absolute_value=True))
                    else:
                        pro_link(V_.tensor_reduce(qmax[:, k:k + 1], RAWQ[:, k], AX_X, ALU.max, apply_absolute_value=True))

                def scales(*_):
                    V_.tensor_reduce(gmax[:, 1:2], qmax[:, :], AX_X, ALU.max).then_inc(s["gmax_in"], 2)
                    dve.wait_ge(s["gmax_all"], 2)
                    power_of_two(gpow[:, 1:3], gall[:, 1:3])
                    pro_link(V_.reciprocal(grec[:, 1:3], gpow[:, 1:3]))
                    pro_link(V_.tensor_scalar(unscale[:, 1:2], gpow[:, 1:2], 2.0 ** -22, None, ALU.mult))
                    pro_link(V_.scalar_tensor_tensor(out=unscale[:, 2:3], in0=gpow[:, 1:2], scalar=2.0 ** -18, in1=gpow[:, 2:3], op0=ALU.mult, op1=ALU.mult))
                    V_.tensor_scalar(gscale[:, 1:3], grec[:, 1:3], 2.0 ** 13, None, ALU.mult).then_inc(s["scales"], 1)
                    dve.wait_ge(s["scales"], 2)

                def weights(out_, k):
                    dve.wait_ge(s["pro_hi"], 1 if out_ else k + 2)
                    W, raw, c = ((WO, RAWO, 2) if out_ else (WQ[:, :, k:k + 1], RAWQ[:, k], 1))
                    V_.scalar_tensor_tensor(out=W[:, 1].rearrange("p k n -> p (k n)"), in0=raw, scalar=gscale[:, c:c + 1],
                                            in1=W[:, 0].rearrange("p k n -> p (k n)"), op0=ALU.mult, op1=ALU.subtract).then_inc(s["pro_lo"], 1)

                run({"magnitude": magnitude, "scales": scales, "weights": weights,
                     "stats": stats, "norm": norm, "split": split, "gated": gated, "parts": parts, "residual": residual,
                     "qkv out": qkv_out, "unit": unit, "stack": stack, "stack out": stack_out, "row max": row_max,
                     "maxima": maxima, "max rows": max_rows, "exp": exp, "y out": y_out, "y turn": y_turn, "out residual": out_residual}, fill)
                assert fill is None or n[0] == LINKS, (n[0], LINKS)

            batch(0, 0, False)
            with dve.Fori(0, B - 1) as it:
                batch(it, 1, True)
            batch(0, B, None)

        @block.tensor
        def _(pe):
            T_ = nc.tensor

            def three(o, lhs, rhs, first, last):
                T_.matmul(o, lhs(0), rhs(0), start=first, stop=False)
                T_.matmul(o, lhs(0), rhs(1), start=False, stop=False)
                return T_.matmul(o, lhs(1), rhs(0), start=False, stop=last)

            pe.wait_ge(s["c_made"], 1)
            for j in range(8):
                pe.wait_ge(s["wscaled"], j + 1)
                if j >= 2:
                    pe.wait_ge(s["w_lo"], 4 * (j - 1))
                for k in range(KC):
                    for i in range(4):
                        ins = T_.transpose(ps((j % 2) * 4 + k, i * P, P), RAW[j % 4][:, i, k * P:(k + 1) * P], ident[:, :])
                ins.then_inc(s["w_tr"], 1)
            pe.wait_ge(s["down_in"], 64)
            pe.wait_ge(s["w_lo"], 32)
            for m in range(16):
                q, t = m // 4, m % 4
                if m >= 8:
                    pe.wait_ge(s["dn_st"], m - 7)
                for i in range(4):
                    ins = T_.transpose(ps(m % 8, i * P, P), RAWD[t][:, (4 * q + i) * P:(4 * q + i + 1) * P], ident[:, :])
                ins.then_inc(s["dn_tr"], 1)
            pe.wait_ge(s["wd_lo"], 4)

            def batch(it, ahead, fill):
                wait = per(pe, it, ahead)
                step = per_step(wait, fill)
                bank3 = [("xt_lo", 12, 10, -1) if fill is not False else None]
                bank2 = [None]
                scored = [None]

                def take(last, *reader):
                    if last[0]:
                        wait(*last[0])
                    last[0] = reader

                def turn(u, t):
                    k, batch = (4 * u + t, 0) if u < 3 else (8 + t, -1)
                    wait("xn_done", 12, k + 1, batch)
                    take(bank3 if turn_bank(u, t) == 3 else bank2, "xt_lo", 12, k + 1, batch)
                    for kc in range(KC):
                        ins = T_.transpose(ps(turn_bank(u, t), kc * P, P), xn[t % 2][:, kc * P:(kc + 1) * P], ident[:, :])
                    ins.then_inc(s["xt_ps"], 1)

                def half_product(f, i, W, at):
                    th, c = i // HC, i % HC
                    for kc in range(KC):
                        ins = three(ps(4 + i % 2, at, TH), lambda q: W[:, q, kc, c * P:(c + 1) * P],
                                    lambda q: XT[f][:, q, kc, th * TH:(th + 1) * TH], kc == 0, kc == KC - 1)
                    return ins

                def gate(f, i):
                    step("gated", f, i, 2)
                    if i % HC == 0:
                        wait("xt_lo", 12, 8 * f + 2 * (i // HC + 1), -f)
                    half_product(f, i, WG, 0)

                def up(f, i):
                    half_product(f, i, WU, TH).then_inc(s["gu_ps"], 1)

                def down(f, i):
                    th, c = i // HC, i % HC
                    step("h_lo", f, i)
                    if c == 0 and th:
                        wait(("x1_done", "out_ready")[f], TT, 2, -f)
                    elif c == 0 and f == 0 and fill:
                        wait("x2_done", TT, TT, -1)
                    for t in range(2):
                        ins = three(ps(6 * f + t), lambda q: HP[i % 2][q][:, t * P:(t + 1) * P], lambda q: WD[:, q, c, :], c == 0, c == HC - 1)
                    ins.then_inc(s["down_done"], 1)

                def qkv(hf, t):
                    i = hf * TT + t
                    if hf == 0:
                        wait("xt_lo", 12, 4 + t + 1)
                    if t:
                        wait("qs_done", 8, i)
                        wait("vlo_done", 8, i)
                    elif hf:
                        wait("phi_done", 32, 2 * HH)
                    else:
                        wait("x1_done", TT, TT)
                    if fill is False and i == 0:
                        wait("pro_lo", 0, 1 + KC)
                        wait("sel_done", 0, 1)
                    for kc in range(KC):
                        ins = three(ps(0).rearrange("p (a n) -> p a n", a=2), lambda q: XT[0][:, q, kc, t * P:(t + 1) * P],
                                    lambda q: WQ[:, q, kc, 0:2 * D].rearrange("p (a n) -> p a n", a=2)[:, :, hf * 256:(hf + 1) * 256], kc == 0, kc == KC - 1)
                    ins.then_inc(s["qk_ps"], 1)
                    for kc in range(KC):
                        ins = three(ps(1, 0, 256), lambda q: XT[0][:, q, kc, t * P:(t + 1) * P],
                                    lambda q: WQ[:, q, kc, 2 * D + hf * 256:2 * D + (hf + 1) * 256], kc == 0, kc == KC - 1)
                    ins.then_inc(s["v_ps"], 1)

                def stack_turn(hf, t):
                    i = hf * TT + t
                    wait("st_lo", 8, i + 1)
                    if i == 0:
                        wait(*bank2[0])
                    elif t:
                        wait("qt_ev", 8, i)
                    for h in range(HH):
                        ins = T_.transpose(ps16(2)[0:ST, h * P:(h + 1) * P], STK[:, h, :], ident16[:, :])
                    ins.then_inc(s["qt_ps"], 1)
                    take(bank3, "kt_ev", 8, i + 1)
                    for h in range(HH):
                        ins = T_.transpose(ps16(3)[0:ST, h * P:(h + 1) * P], STK[:, HH + h, :], ident16[:, :])
                    ins.then_inc(s["kt_ps"], 1)

                def bank_free(bank):
                    if scored[0]:
                        name, k = scored[0]
                        if name == "smax_done":
                            wait(name, 48, 3 * k + bank + 1)
                        else:
                            wait(name, 32, 2 * k + min(bank, 1) + 1)

                def scores_max(hf, h):
                    k = hf * HH + h
                    if h == 0:
                        wait("qt_ev", 8, (hf + 1) * TT)
                        wait("kt_ev", 8, (hf + 1) * TT)
                        scored[0] = None
                    for bank, tiles in enumerate(QBANKS):
                        bank_free(bank)
                        for t in tiles:
                            w = (t + 1) * P
                            T_.matmul(ps(0, QSEG[t], w), QT[0:ST, h, t * P:(t + 1) * P], KT[0:ST, h, 0:w], start=True, stop=False)
                            ins = T_.matmul(ps(0, QSEG[t] + t * P, P), identb[:, :], maskq[:, :], start=False, stop=True)
                        ins.then_inc(s["s1_ps"], 1)
                    scored[0] = ("smax_done", k)

                def max_rows(hf, g):
                    wait("mst_done", 4, hf * 2 + g + 1)
                    take(bank3, "mt_copied", 4, hf * 2 + g + 1)
                    for t in range(TT):
                        ins = T_.transpose(ps16(3)[ST:ST + MR, t * P:(t + 1) * P], mst[:, t * MR:(t + 1) * MR], ident16[:, :])
                    ins.then_inc(s["mt_ps"], 1)

                def scores(hf, h):
                    k = hf * HH + h
                    if h % GH == 0:
                        wait("mt_copied", 4, k // GH + 1)
                    elif h % GH == 1:
                        wait("mrow_done", 4, k // GH + 1)
                    for bank, tiles in enumerate(KBANKS):
                        bank_free(bank)
                        for t in tiles:
                            w = (TT - t) * P
                            T_.matmul(ps(0, KSEG[t], w), KT[0:ST + MR, h, t * P:(t + 1) * P], QT[0:ST + MR, h, t * P:S], start=True, stop=False)
                            ins = T_.matmul(ps(0, KSEG[t], P), identb[:, :], maskk[:, :], start=False, stop=True)
                        if bank != 1:
                            ins.then_inc(s["s2_ps"], 1)
                    scored[0] = ("phi_done", k)

                def values(hf, h):
                    k = hf * HH + h
                    wait("plo_done", 32, 2 * (k + 1))
                    take(bank3, "y_read", 16, k + 1)
                    for t in range(TT):
                        for kt in range(t + 1):
                            c = KSEG[kt] + (t - kt) * P
                            T_.matmul(ps(3, t * YW, YW), PHI[:, c:c + P], V[:, kt, h, 0:YW], start=kt == 0, stop=False)
                            ins = T_.matmul(ps(3, t * YW + HD, HD + 1), PLO[:, c:c + P], V[:, kt, h, HD:YW], start=False, stop=kt == t)
                    ins.then_inc(s["pv_ps"], 1)

                def y_turn(hf, g):
                    k = hf * 2 + g
                    wait("ynorm_done", 16, GH * (k + 1))
                    take(bank3, "yt_lo", 4, k + 1)
                    for t in range(TT):
                        ins = T_.transpose(ps(3, t * P, P), Yf[g][:, t].rearrange("p h c -> p (h c)"), ident[:, :])
                    ins.then_inc(s["yt_ps"], 1)

                def out_chunks(t, chunks):
                    for kc in chunks:
                        ins = three(ps(t % 3), lambda q: YT[kc // 2][:, q, kc % 2, t * P:(t + 1) * P], lambda q: WO[:, q, kc, :], kc == 0, kc == KC - 1)
                    return ins

                def out_part(_, t):
                    if t == 3:
                        wait("x2_done", TT, 1)
                    elif t == 0:
                        wait("yt_lo", 4, 3)
                        wait("phi_done", 32, 32)
                    out_chunks(t, range(KC - 1))

                def out_product(_, t):
                    wait("yt_lo", 4, 4)
                    out_chunks(t, [KC - 1]).then_inc(s["op_ps"], 1)

                run({"turn": turn, "gate": gate, "up": up, "down": down, "qkv": qkv, "stack turn": stack_turn, "scores max": scores_max,
                     "max rows": max_rows, "scores": scores, "values": values, "y turn": y_turn,
                     "out part": out_part, "out": out_product}, fill)

            batch(0, 0, False)
            with pe.Fori(0, B - 1) as it:
                batch(it, 1, True)
            batch(0, B, None)


_INS = ["L0_attn_x", "L0_attn_w_qkv", "L0_attn_w_out", "L0_attn_q_gain", "L0_ffn_w_gate", "L0_ffn_w_up", "L0_ffn_w_down"]


def rope_table():
    import numpy as np
    half = HD // 2
    freq = np.float32(10000.0) ** (-np.arange(half, dtype=np.float32) / np.float32(half))
    theta = np.arange(S, dtype=np.float32)[:, None] * freq[None, :]
    c, sn = np.cos(theta), np.sin(theta)
    return np.concatenate([c, c, -sn, sn], axis=1).astype(np.float32)


def kernel(**inputs):
    import numpy as np
    import concourse.bacc as bacc
    from concourse.bass_utils import run_bass_kernel_spmd

    nc = bacc.Bacc("TRN2", target_bir_lowering=False, num_devices=1)
    arrays, args = {}, []
    for name in _INS:
        a = np.ascontiguousarray(inputs[name])
        arrays[f"in_{name}"] = a
        args.append(nc.dram_tensor(f"in_{name}", a.shape, F32, kind="ExternalInput").ap())
    arrays["rope_table"] = rope_table()
    args.append(nc.dram_tensor("rope_table", (S, 64), F32, kind="ExternalInput").ap())
    args.append(nc.dram_tensor("out", (B, S, D), F32, kind="ExternalOutput").ap())
    build(nc, *args)
    r = run_bass_kernel_spmd(nc, [arrays], core_ids=[0])
    return r.results[0]["out"]
```
